# Optimizing a Trainium2 kernel written in Bass

```python
import numpy as np
import jax
import jax.numpy as jnp

def _softmax(x, axis=-1):
    return jax.nn.softmax(x, axis=axis)

def _gelu(x):
    return jax.nn.gelu(x, approximate=True)

def _silu(x):
    return jax.nn.silu(x)

def _sigmoid(x):
    return jax.nn.sigmoid(x)

def _layernorm(x, axis=-1, eps=1e-05):
    m = jnp.mean(x, axis=axis, keepdims=True)
    v = jnp.var(x, axis=axis, keepdims=True)
    return (x - m) / jnp.sqrt(v + eps)

def _scatter_add(tgt, idx, src, axis=0):
    return tgt.at[idx].add(src)

def _segment_sum(src, seg, n):
    return jax.ops.segment_sum(src, seg, n)
kernel_name = 'mk_xattn_ffn_d1_seqx_r4_bdc38b'

def setup_inputs(seed: int=0):
    np.random.seed(seed)
    _w = jnp.asarray

    def _rec_inputs():
        import jax
        import jax.numpy as jnp
        _rk = jax.random.key(seed)
        x = -0.0003929 + 0.9999 * jax.random.normal(jax.random.fold_in(_rk, 1), (8, 100, 256), jnp.float32)
        _lenS = 100 - jax.random.randint(jax.random.fold_in(_rk, 7), (8,), 0, max(1, 100 // 4) + 1, jnp.int32)
        _lenS2 = 361 - jax.random.randint(jax.random.fold_in(_rk, 8), (8,), 0, max(1, 361 // 4) + 1, jnp.int32)
        _ctx_1024P = jax.random.normal(jax.random.fold_in(_rk, 11), (8, 16, 256), jnp.float32)
        _ctx_1024c = jax.random.dirichlet(jax.random.fold_in(_rk, 511), 0.3 * jnp.ones((16,), jnp.float32), (8, 361))
        _ctx_1024t = jnp.einsum('bsk,bkd->bsd', _ctx_1024c, _ctx_1024P)
        _ctx_1024t = _ctx_1024t * jax.lax.rsqrt(jnp.mean(jnp.square(_ctx_1024t)) + 1e-12) * 0.953939
        ctx_1024 = 2.81802e-05 + 1.00001 * (_ctx_1024t + 0.3 * jax.random.normal(jax.random.fold_in(_rk, 611), (8, 361, 256), jnp.float32))
        return (x, ctx_1024)
    x, ctx_1024 = _rec_inputs()

    def _L0_xattn_setup():
        import jax, jax.numpy as jnp
        import numpy as np
        E = 256
        NUM_HEADS = 16
        DK = E // NUM_HEADS
        EPS = 1e-05
        NEG_INF = -jnp.inf

        def layer_norm(x, g, b):
            mu = jnp.mean(x, axis=-1, keepdims=True)
            var = jnp.var(x, axis=-1, keepdims=True)
            return (x - mu) * jax.lax.rsqrt(var + EPS) * g + b

        def self_attn(x, Wq, Wk, Wv):
            Q, K, V = (x @ Wq, x @ Wk, x @ Wv)
            energy = jnp.einsum('bqd,bkd->bqk', Q, K)
            S = energy.shape[-1]
            lengths = jnp.sum(energy[:, 0] != 0, axis=-1)
            kidx = jnp.arange(S)
            pad = kidx[None, None, :] >= lengths[:, None, None]
            causal = kidx[None, :] < kidx[:, None]
            causal = (kidx[None, :] > kidx[:, None])[None]
            energy = jnp.where(pad | causal, NEG_INF, energy)
            score = jax.nn.softmax(energy / np.sqrt(DK), axis=-1)
            return jnp.einsum('bqk,bkd->bqd', score, V)

        def cross_attn(x, context, Wq, Wk, Wv):
            Q = x @ Wq
            K, V = (context @ Wk, context @ Wv)
            energy = jnp.einsum('bqd,bkd->bqk', Q, K)
            Sk = energy.shape[-1]
            lengths = jnp.sum(energy[:, 0] != 0, axis=-1)
            kidx = jnp.arange(Sk)
            pad = kidx[None, None, :] >= lengths[:, None, None]
            energy = jnp.where(pad, NEG_INF, energy)
            score = jax.nn.softmax(energy / np.sqrt(DK), axis=-1)
            return jnp.einsum('bqk,bkd->bqd', score, V)
        key = jax.random.key(seed)
        ks = jax.random.split(key, 12)
        B, S = (8, 512)
        s = 1.0 / np.sqrt(E)
        inp = {'x': jax.random.normal(ks[0], (B, S, E), jnp.float32), 'context': jax.random.normal(ks[1], (B, S, E), jnp.float32), 'Wq1': jax.random.normal(ks[2], (E, E), jnp.float32) * s, 'Wk1': jax.random.normal(ks[3], (E, E), jnp.float32) * s, 'Wv1': jax.random.normal(ks[4], (E, E), jnp.float32) * s, 'Wq2': jax.random.normal(ks[5], (E, E), jnp.float32) * s, 'Wk2': jax.random.normal(ks[6], (E, E), jnp.float32) * s, 'Wv2': jax.random.normal(ks[7], (E, E), jnp.float32) * s, 'fc1_w': jax.random.normal(ks[8], (E, E), jnp.float32) * s, 'fc1_b': jnp.zeros((E,), jnp.float32), 'fc2_w': jax.random.normal(ks[9], (E, E), jnp.float32) * s, 'fc2_b': jnp.zeros((E,), jnp.float32), 'ln1_g': jnp.ones((E,), jnp.float32), 'ln1_b': jnp.zeros((E,), jnp.float32), 'ln2_g': jnp.ones((E,), jnp.float32), 'ln2_b': jnp.zeros((E,), jnp.float32), 'ln3_g': jnp.ones((E,), jnp.float32), 'ln3_b': jnp.zeros((E,), jnp.float32)}
        return inp
    _L0_xattn_all = _L0_xattn_setup()
    _L0_xattn_in = {k: v for k, v in _L0_xattn_all.items() if k in ('Wq1', 'Wk1', 'Wv1', 'Wq2', 'Wk2', 'Wv2', 'fc1_w', 'fc1_b', 'fc2_w', 'fc2_b', 'ln1_g', 'ln1_b', 'ln2_g', 'ln2_b', 'ln3_g', 'ln3_b')}
    del _L0_xattn_all

    def _L0_ffn_setup():
        import jax, jax.numpy as jnp
        import numpy as np
        B, S, D = (4, 1024, 256)
        E, F_EXP = (16, 512)
        F_C = 2.0
        F_SH = 512
        key = jax.random.key(seed)
        ks = jax.random.split(key, 8)
        s = 0.02
        return {'hidden_states': jax.random.normal(ks[0], (B, S, D), jnp.float32), 'gate_w': jax.random.normal(ks[1], (E, D), jnp.float32) * s, 'Wg': jax.random.normal(ks[2], (E, F_EXP, D), jnp.float32) * s, 'Wu': jax.random.normal(ks[3], (E, F_EXP, D), jnp.float32) * s, 'Wd': jax.random.normal(ks[4], (E, D, F_EXP), jnp.float32) * s, 'Ws_g': jax.random.normal(ks[5], (F_SH, D), jnp.float32) * s, 'Ws_u': jax.random.normal(ks[6], (F_SH, D), jnp.float32) * s, 'Ws_d': jax.random.normal(ks[7], (D, F_SH), jnp.float32) * s}
    _L0_ffn_all = _L0_ffn_setup()
    _L0_ffn_in = {k: v for k, v in _L0_ffn_all.items() if k in ('gate_w', 'Wg', 'Wu', 'Wd', 'Ws_g', 'Ws_u', 'Ws_d')}
    del _L0_ffn_all
    return {'x': x, 'ctx_1024': ctx_1024, 'L0_xattn_Wq1': _L0_xattn_in['Wq1'], 'L0_xattn_Wk1': _L0_xattn_in['Wk1'], 'L0_xattn_Wv1': _L0_xattn_in['Wv1'], 'L0_xattn_Wq2': _L0_xattn_in['Wq2'], 'L0_xattn_Wk2': _L0_xattn_in['Wk2'], 'L0_xattn_Wv2': _L0_xattn_in['Wv2'], 'L0_xattn_fc1_w': _L0_xattn_in['fc1_w'], 'L0_xattn_fc1_b': _L0_xattn_in['fc1_b'], 'L0_xattn_fc2_w': _L0_xattn_in['fc2_w'], 'L0_xattn_fc2_b': _L0_xattn_in['fc2_b'], 'L0_xattn_ln1_g': _L0_xattn_in['ln1_g'], 'L0_xattn_ln1_b': _L0_xattn_in['ln1_b'], 'L0_xattn_ln2_g': _L0_xattn_in['ln2_g'], 'L0_xattn_ln2_b': _L0_xattn_in['ln2_b'], 'L0_xattn_ln3_g': _L0_xattn_in['ln3_g'], 'L0_xattn_ln3_b': _L0_xattn_in['ln3_b'], 'L0_ffn_gate_w': _L0_ffn_in['gate_w'], 'L0_ffn_Wg': _L0_ffn_in['Wg'], 'L0_ffn_Wu': _L0_ffn_in['Wu'], 'L0_ffn_Wd': _L0_ffn_in['Wd'], 'L0_ffn_Ws_g': _L0_ffn_in['Ws_g'], 'L0_ffn_Ws_u': _L0_ffn_in['Ws_u'], 'L0_ffn_Ws_d': _L0_ffn_in['Ws_d']}

def reference(x, ctx_1024, L0_xattn_Wq1, L0_xattn_Wk1, L0_xattn_Wv1, L0_xattn_Wq2, L0_xattn_Wk2, L0_xattn_Wv2, L0_xattn_fc1_w, L0_xattn_fc1_b, L0_xattn_fc2_w, L0_xattn_fc2_b, L0_xattn_ln1_g, L0_xattn_ln1_b, L0_xattn_ln2_g, L0_xattn_ln2_b, L0_xattn_ln3_g, L0_xattn_ln3_b, L0_ffn_gate_w, L0_ffn_Wg, L0_ffn_Wu, L0_ffn_Wd, L0_ffn_Ws_g, L0_ffn_Ws_u, L0_ffn_Ws_d):
    import jax
    import jax.numpy as jnp

    def _L0_xattn_ref(x, context, Wq1, Wk1, Wv1, Wq2, Wk2, Wv2, fc1_w, fc1_b, fc2_w, fc2_b, ln1_g, ln1_b, ln2_g, ln2_b, ln3_g, ln3_b):
        import jax, jax.numpy as jnp
        import numpy as np
        E = 256
        NUM_HEADS = 16
        DK = E // NUM_HEADS
        EPS = 1e-05
        NEG_INF = -jnp.inf

        def layer_norm(x, g, b):
            mu = jnp.mean(x, axis=-1, keepdims=True)
            var = jnp.var(x, axis=-1, keepdims=True)
            return (x - mu) * jax.lax.rsqrt(var + EPS) * g + b

        def self_attn(x, Wq, Wk, Wv):
            Q, K, V = (x @ Wq, x @ Wk, x @ Wv)
            energy = jnp.einsum('bqd,bkd->bqk', Q, K)
            S = energy.shape[-1]
            lengths = jnp.sum(energy[:, 0] != 0, axis=-1)
            kidx = jnp.arange(S)
            pad = kidx[None, None, :] >= lengths[:, None, None]
            causal = kidx[None, :] < kidx[:, None]
            causal = (kidx[None, :] > kidx[:, None])[None]
            energy = jnp.where(pad | causal, NEG_INF, energy)
            score = jax.nn.softmax(energy / np.sqrt(DK), axis=-1)
            return jnp.einsum('bqk,bkd->bqd', score, V)

        def cross_attn(x, context, Wq, Wk, Wv):
            Q = x @ Wq
            K, V = (context @ Wk, context @ Wv)
            energy = jnp.einsum('bqd,bkd->bqk', Q, K)
            Sk = energy.shape[-1]
            lengths = jnp.sum(energy[:, 0] != 0, axis=-1)
            kidx = jnp.arange(Sk)
            pad = kidx[None, None, :] >= lengths[:, None, None]
            energy = jnp.where(pad, NEG_INF, energy)
            score = jax.nn.softmax(energy / np.sqrt(DK), axis=-1)
            return jnp.einsum('bqk,bkd->bqd', score, V)
        z = self_attn(x, Wq1, Wk1, Wv1)
        x = layer_norm(x + z, ln1_g, ln1_b)
        z = cross_attn(x, context, Wq2, Wk2, Wv2)
        x = layer_norm(x + z, ln2_g, ln2_b)
        z = jax.nn.relu(x @ fc1_w + fc1_b)
        z = z @ fc2_w + fc2_b
        return layer_norm(x + z, ln3_g, ln3_b)

    def _L0_ffn_ref(hidden_states, gate_w, Wg, Wu, Wd, Ws_g, Ws_u, Ws_d):
        import jax, jax.numpy as jnp
        import numpy as np
        B, S, D = (4, 1024, 256)
        E, F_EXP = (16, 512)
        F_C = 2.0
        F_SH = 512
        b, s, d = hidden_states.shape
        e = gate_w.shape[0]
        cap = int(s * F_C / e)
        logits = jnp.einsum('bsd,ed->bse', hidden_states, gate_w)
        scores = jax.nn.softmax(logits, axis=-1).transpose(0, 2, 1)
        topk_w, topk_idx = jax.lax.top_k(scores, cap)
        x_tok = jnp.take_along_axis(hidden_states[:, None, :, :], topk_idx[..., None], axis=2)
        g = jnp.einsum('becd,efd->becf', x_tok, Wg)
        u = jnp.einsum('becd,efd->becf', x_tok, Wu)
        h = jax.nn.gelu(g, approximate=False) * u
        eo = jnp.einsum('becf,edf->becd', h, Wd) * topk_w[..., None]
        offs = (jnp.arange(b) * s)[:, None, None]
        flat_idx = (topk_idx + offs).reshape(-1)
        flat = jnp.zeros((b * s, d), hidden_states.dtype)
        flat = flat.at[flat_idx].add(eo.reshape(-1, d))
        out = flat.reshape(b, s, d)
        gs = jnp.einsum('bsd,fd->bsf', hidden_states, Ws_g)
        us = jnp.einsum('bsd,fd->bsf', hidden_states, Ws_u)
        shared = jnp.einsum('bsf,df->bsd', jax.nn.gelu(gs, approximate=False) * us, Ws_d)
        return out + shared
    x = x + _L0_xattn_ref(_layernorm(x, axis=-1), ctx_1024, L0_xattn_Wq1, L0_xattn_Wk1, L0_xattn_Wv1, L0_xattn_Wq2, L0_xattn_Wk2, L0_xattn_Wv2, L0_xattn_fc1_w, L0_xattn_fc1_b, L0_xattn_fc2_w, L0_xattn_fc2_b, L0_xattn_ln1_g, L0_xattn_ln1_b, L0_xattn_ln2_g, L0_xattn_ln2_b, L0_xattn_ln3_g, L0_xattn_ln3_b)
    x = x + _L0_ffn_ref(_layernorm(x, axis=-1), L0_ffn_gate_w, L0_ffn_Wg, L0_ffn_Wu, L0_ffn_Wd, L0_ffn_Ws_g, L0_ffn_Ws_u, L0_ffn_Ws_d)
    return x

_drawn_inputs = setup_inputs


def setup_inputs(seed=0):
    import zlib

    import numpy as np

    out = dict(_drawn_inputs(seed))
    spreads = {'L0_xattn_fc1_b': (0.0, 0.274),
     'L0_xattn_fc2_b': (0.0, 0.1),
     'L0_xattn_ln1_g': (1.0, 0.2),
     'L0_xattn_ln1_b': (0.0, 0.1),
     'L0_xattn_ln2_g': (1.0, 0.2),
     'L0_xattn_ln2_b': (0.0, 0.1),
     'L0_xattn_ln3_g': (1.0, 0.2),
     'L0_xattn_ln3_b': (0.0, 0.1)}
    factors = {'L0_ffn_gate_w': 8.0,
     'L0_ffn_Wg': 8.0,
     'L0_ffn_Wu': 8.0,
     'L0_ffn_Wd': 8.0,
     'L0_ffn_Ws_g': 4.076,
     'L0_ffn_Ws_u': 3.968,
     'L0_ffn_Ws_d': 3.965}
    for name, (base, spread) in spreads.items():
        noise = np.random.default_rng([zlib.crc32(name.encode()), seed]).standard_normal(out[name].shape)
        drawn = base * np.exp(spread * noise) if base else spread * noise
        out[name] = jnp.asarray(drawn.astype(out[name].dtype))
    for name, factor in factors.items():
        out[name] = (out[name] * factor).astype(out[name].dtype)
    return out
```

```python
from contextlib import ExitStack

import concourse.bass as bass
from concourse import mybir

ALU = mybir.AluOpType
ACT = mybir.ActivationFunctionType
AX = mybir.AxisListType
F32 = mybir.dt.float32
BF16 = mybir.dt.bfloat16
U32 = mybir.dt.uint32

P = 128
B, T, D = 8, 100, 256
S = 361
NT = B * T
KD = D // P
KS = -(-S // P)
SP_ = KS * P
PAIRS = B // 2
E, F = 16, 512
KF = F // P
CAP = int(T * 2.0 / E)
SLOTS = B * CAP
HALF = E // 2
EC = E * CAP
INV_SQRT_DK = 1.0 / (D // 16) ** 0.5
EPS = 1e-5
FAR = -3.0e38
WE = 2 * KD * F + KF * D
RING = 4
BANKS = 8

C_IDENT = 0
C_CAUSAL = C_IDENT + P
C_KEY = C_CAUSAL + T
C_ROW = C_KEY + S
C_EMASK = C_ROW + 1
C_BATCH = C_EMASK + E
C_ONES = C_BATCH + B
C_VEC = C_ONES + T
C_END = C_VEC + 5 * KD
V_G1, V_B1, V_G2, V_B2, V_FC1 = (C_VEC + KD * i for i in range(5))
R_G1, R_B1, R_G2, R_B2, R_G3, R_B3, R_FC2 = range(7)
W_Q1T, W_K1T, W_V1, W_Q2T, W_K2T, W_V2, W_FC1, W_FC2 = range(8)

CHAIN = [
    (0, ["ln0", "xT", "gT", "v"]),
    (1, ["e1", "len1", "soft1"]),
    (2, ["p1T", "z1", "ln1"]),
    (3, ["x1T", "g2T"]),
    (4, ["e2", "len2", "soft2"]),
    (5, ["p2T", "uT"]),
    (6, ["z2", "ln2"]),
    (7, ["x2T", "f1"]),
    (8, ["f2", "ln3"]),
    (9, ["ln4", "hT"]),
    (10, ["route", "sh"]),
]


def order():
    steps = max(lag for lag, _ in CHAIN) + PAIRS
    out = []
    for step in range(steps):
        for j in range(PAIRS):
            for lag, stages in CHAIN:
                if step - j == lag:
                    out += [(s, j) for s in stages]
    return out


BANKS_OF = {"m": 1, "xT": 1, "gT": 1, "v": 1, "e1": 1, "p1T": 1, "z1": 1, "x1T": 1, "g2T": 1, "e2": 2,
            "p2T": 2, "uT": 1, "z2": 1, "x2T": 1, "f1": 1, "f2": 1, "hT": 1, "sh": 4}


def xattn_moe(nc, x, ctx_tok, ctx_feat, w_small, consts, rows, gate, w_moe, out):
    stack = ExitStack()
    with stack:
        def sb(name, shape, dt=F32):
            return stack.enter_context(nc.sbuf_tensor(name, shape, dt))

        def sem(name):
            return stack.enter_context(nc.semaphore(name))

        cst = sb("cst", [P, C_END])
        row = sb("row", [P, 7, D])
        wsm = sb("wsm", [P, 8, KD, D])
        m1 = wsm[:, W_Q1T]
        m2 = wsm[:, W_Q2T]
        gate_sb = sb("gate_sb", [P, KD, E])
        xres = sb("xres", [T, B, D])
        xn = sb("xn", [T, B, D])
        featA = sb("featA", [P, KD, NT])
        featB = sb("featB", [P, KD, NT])
        vbuf = sb("vbuf", [T, B, D])
        rn = sb("rn", [T, 2, B, D])
        x1 = sb("x1", [T, B, D])
        masks = sb("masks", [P, 2, 2, S])
        pen = masks[0:T, 0]
        emk = masks[0:T, 1]
        probs = sb("probs", [P, 2, B, T])
        p1 = probs[0:T, 0]
        p1T = probs[0:T, 1]
        cross = sb("cross", [P, 4, SP_])
        p2 = cross[0:T]
        p2T = sb("p2T", [P, 4, KS, T])
        uT = sb("uT", [P, KD, NT])
        CR = 4
        region = sb("region", [P, CR * (KS * D + KD * S) + 400])
        ctxk = region[:, 0:CR * KS * D].rearrange("p (b c d) -> p b c d", b=CR, c=KS)
        ctxf = region[:, CR * KS * D:CR * (KS * D + KD * S)].rearrange("p (b k s) -> p b k s", b=CR, k=KD)
        we = sb("we", [P, RING, WE])
        wshared = sb("wshared", [P, WE])
        st6 = sb("st6", [T, 5, B, 6])
        mv = sb("mv", [T, 5, B, 2])
        ve = sb("ve", [T, 5, B, 1])
        rstd = sb("rstd", [T, 5, B, 1])
        nhalf = sb("nhalf", [T, 2, 1])
        nz = sb("nz", [1, S])
        cnt = sb("cnt", [1, 2, B])
        nmax = sb("nmax", [T, 2, B])
        rsum = sb("rsum", [T, 2, B])
        rinv = sb("rinv", [T, 2, B])
        linv = sb("linv", [T, 2, B])
        hs = region[:, 0:KF * NT].rearrange("p (f t) -> p f t", f=KF)
        xg = region[:, KF * NT:KF * NT + KD * E * SLOTS].rearrange("p (k e s) -> p k e s", k=KD, e=E)
        eo_all = rn[0:HALF * CAP]
        sel = vbuf[:].rearrange("t b d -> t (b d)")[:, 0:B * EC].rearrange("t (b c) -> t b c", b=B)
        wsel = x1[:].rearrange("t b d -> t (b d)")[0:HALF * CAP, 0:2 * B * T].rearrange(
            "p (h b t) -> p h b t", h=2, b=B)
        late = probs[:].rearrange("p a b t -> p (a b t)")
        gel = late[:, 0:2 * 4 * T].rearrange("p (r c) -> p r c", r=2)
        eo = late[0:SLOTS, 2 * 4 * T:2 * 4 * T + 2 * D].rearrange("p (r d) -> p r d", r=2)
        hE = masks[:].rearrange("p a b s -> p (a b s)")[:, 0:2 * KF * SLOTS].rearrange("p (r c) -> p r c", r=2)
        lmx = sb("lmx", [T, B])
        gate_rows = vbuf[:].rearrange("t b d -> t (b d)")[:, B * EC:B * EC + 3 * B * E].rearrange(
            "t (a b e) -> t a b e", a=3, b=B)
        lsh = gate_rows[:, 0]
        lex = gate_rows[:, 1]
        score = gate_rows[:, 2]
        lsum = sb("lsum", [T, B])
        lri = sb("lri", [T, B])
        sS = sb("sS", [P, T])
        sS2 = sb("sS2", [P, T])
        top = sb("top", [P, 16])
        tix = sb("tix", [P, 16], U32)
        tixf = sb("tixf", [P, 16])
        dix = sb("dix", [P, E, CAP], BF16)
        dw = cross[:, 0, 0:EC].rearrange("p (e c) -> p e c", e=E)
        bsel = sb("bsel", [P, B, T], BF16)
        bcol = sb("bcol", [P, B], BF16)
        wcol = sb("wcol", [HALF * CAP, 2, 2, B])

        psum = stack.enter_context(nc.psum_tensor("psum", [P, BANKS, 512], F32))

        ident = cst[:, C_IDENT:C_IDENT + P]

        d_x = sem("d_x")
        d_w = sem("d_w")
        d_cst = sem("d_cst")
        d_row = sem("d_row")
        d_ck = [sem(f"d_ck{i}") for i in range(PAIRS)]
        d_gate = sem("d_gate")
        d_sh = sem("d_sh")
        d_we = [sem(f"d_we{i}") for i in range(RING)]
        d_eo = [sem(f"d_eo{i}") for i in range(2)]
        d_out = sem("d_out")
        pe_m, act_m = sem("pe_m"), sem("act_m")
        k_dve, k_pool = sem("k_dve"), sem("k_pool")
        s_const = sem("s_const")
        pe = {s: sem("pe_" + s) for s in ("xT", "gT", "v", "e1", "len1", "p1T", "z1", "x1T", "g2T", "e2", "len2",
                                          "p2T", "uT", "z2", "x2T", "f1", "f2", "hT", "lg", "sc", "bc", "col", "gather", "shG", "shU", "shD",
                                          "G", "U", "eo", "scat")}
        cp = {s: sem("cp_" + s) for s in ("xT", "gT", "v", "p1T", "x1T", "g2T", "p2T", "uT", "x2T", "f1", "hT")}
        s_mv = [sem(f"s_mv{i}") for i in range(5)]
        s_rs = [sem(f"s_rs{i}") for i in range(5)]
        s_n = [sem(f"s_n{i}") for i in range(5)]
        s_cnt = [sem("s_cnt1"), sem("s_cnt2")]
        s_mask = [sem("s_mask1"), sem("s_mask2")]
        s_exp = [sem("s_exp1"), sem("s_exp2")]
        s_r = [None, sem("s_r1"), sem("s_r2"), sem("s_r3")]
        s_x1, s_x2, s_x3, s_xb = sem("s_x1"), sem("s_x2"), sem("s_x3"), sem("s_xb")
        s_gel, s_hs = sem("s_gel"), sem("s_hs")
        s_lsh, s_lex, s_score, s_S, s_dd, s_sel, s_col, s_wsel, s_xg = (
            sem(n) for n in ("s_lsh", "s_lex", "s_score", "s_S", "s_dd", "s_sel", "s_col", "s_wsel", "s_xg"))
        s_egel, s_eh, s_eo, s_y, s_fin = sem("s_egel"), sem("s_eh"), sem("s_eo"), sem("s_y"), sem("s_fin")

        ORDER = order()

        def freed_by(stage, j, i):
            table = {"m": (act_m, 2), "xT": (cp["xT"], j + 1), "gT": (cp["gT"], j + 1), "v": (cp["v"], j + 1),
                     "e1": (s_mask[0], j + 1), "p1T": (cp["p1T"], j + 1), "z1": (s_r[1], j + 1),
                     "x1T": (cp["x1T"], j + 1), "g2T": (cp["g2T"], j + 1), "e2": (s_mask[1], 2 * j + i + 1),
                     "p2T": (cp["p2T"], 2 * j + i + 1), "uT": (cp["uT"], j + 1), "z2": (s_r[2], j + 1),
                     "x2T": (cp["x2T"], j + 1), "f1": (cp["f1"], j + 1), "f2": (s_r[3], j + 1),
                     "hT": (cp["hT"], j + 1),
                     "sh": (s_gel if i % 2 == 0 else s_hs, 2 * j + i // 2 + 1)}
            return table[stage]

        turns = [("m", 0, 0)]
        for s_, j_ in ORDER:
            turns += [(s_, j_, i) for i in range(BANKS_OF.get(s_, 0))]
            if s_ == "route" and j_ == PAIRS - 1:
                turns += [("lg", 0, 0)]
        turn_no = {t: n for n, t in enumerate(turns)}

        def bank(stage, j, i=0):
            return psum[:, turn_no[(stage, j, i)] % BANKS, :]

        def take_bank(eng, stage, j, i=0):
            n = turn_no[(stage, j, i)]
            if n >= BANKS:
                last = turns[n - BANKS]
                eng.wait_ge(*(freed_by(*last) if last[0] != "lg" else (s_lsh, 1)))
            return psum[:, n % BANKS, :]

        def gbank(e):
            return psum[:, e % 2, :]

        def ubank(e):
            return psum[:, 2 + e % 2, :]

        def obank(e):
            return psum[:, 4 + e % 2, :]

        def dbank(n):
            return psum[:, 6 + n % 2, :]

        def toks(j, i):
            return slice((2 * j + i) * T, (2 * j + i + 1) * T)

        def pair_cols(j):
            return slice(2 * j * T, (2 * j + 2) * T)

        def bcast_row(r, n=2):
            return row[0:T, r, :].unsqueeze(1).to_broadcast([T, n, D])

        block = stack.enter_context(nc.Block())

        @block.sync
        def _(sp):
            xv = x.rearrange("b t d -> t b d")
            sp.dma_start(xres[:, 0:2, :], xv[:, 0:2, :]).then_inc(d_x, 16)
            sp.dma_start(cst[:], consts).then_inc(d_cst, 16)
            sp.dma_start(wsm[:, 0:3], w_small[:, 0:3]).then_inc(d_w, 16)
            for j in range(1, PAIRS):
                sp.wait_ge(d_x, 16 * j)
                sp.dma_start(xres[:, 2 * j:2 * j + 2, :], xv[:, 2 * j:2 * j + 2, :]).then_inc(d_x, 16)
            sp.wait_ge(d_w, 16)
            sp.dma_start(wsm[:, 3:8], w_small[:, 3:8]).then_inc(d_w, 16)
            sp.dma_start(row[:], rows.partition_broadcast(P)).then_inc(d_row, 16)

            def load_ctx(j):
                c = 2 * j % CR
                if 2 * j >= CR:
                    sp.wait_ge(pe["uT"], j - CR // 2 + 1)
                sp.dma_start(ctxf[:, c:c + 2], ctx_feat[:, 2 * j:2 * j + 2]).then_inc(d_ck[j], 16)
                sp.dma_start(ctxk[:, c:c + 2], ctx_tok[:, 2 * j:2 * j + 2]).then_inc(d_ck[j], 16)

            def load_expert(e):
                if e >= RING:
                    sp.wait_ge(pe["eo"], e - RING + 1)
                sp.dma_start(we[:, e % RING], w_moe[e]).then_inc(d_we[e % RING], 16)

            load_ctx(0)
            load_ctx(1)
            sp.dma_start(gate_sb[:], gate).then_inc(d_gate, 16)
            sp.dma_start(wshared[:], w_moe[E]).then_inc(d_sh, 16)
            load_expert(0)
            load_ctx(2)
            load_ctx(3)
            for e in range(1, RING):
                load_expert(e)

            for e in range(E):
                if e + RING < E:
                    load_expert(e + RING)
                sp.wait_ge(s_eo, e + 1)
                r0 = (e % HALF) * CAP
                for b in range(B):
                    sp.dma_start(eo_all[r0:r0 + CAP, e // HALF, b, :],
                                 eo[b * CAP:(b + 1) * CAP, e % 2, :]).then_inc(d_eo[e % 2], 16)

            ov = out.rearrange("b t d -> t b d")
            for j in range(PAIRS):
                sp.wait_ge(s_fin, j + 1)
                sp.dma_start(ov[:, 2 * j:2 * j + 2, :], xres[:, 2 * j:2 * j + 2, :]).then_inc(d_out, 16)
            sp.wait_ge(d_out, 16 * PAIRS)

        @block.tensor
        def _(eng):
            mm = nc.tensor.matmul

            def transposes(stage, j, src, ready):
                eng.wait_ge(*ready)
                ps = take_bank(eng, stage, j)
                for k in range(KD):
                    for i in range(2):
                        c0 = (2 * k + i) * T
                        last = nc.tensor.transpose(ps[:, c0:c0 + T], src[:, 2 * j + i, k * P:(k + 1) * P],
                                                   ident[0:T, 0:T])
                last.then_inc(pe[stage], 1)

            def feature_product(stage, j, w, rhs, ready):
                eng.wait_ge(*ready)
                ps = take_bank(eng, stage, j)
                for m in range(KD):
                    for k in range(KD):
                        last = mm(ps[:, 2 * m * T:2 * (m + 1) * T], w[:, k, m * P:(m + 1) * P],
                                  rhs[:, k, pair_cols(j)], start=(k == 0), stop=(k == KD - 1))
                last.then_inc(pe[stage], 1)

            def token_product(stage, j, lhs, w, ready):
                eng.wait_ge(*ready)
                ps = take_bank(eng, stage, j)
                for i in range(2):
                    for k in range(KD):
                        last = mm(ps[0:T, i * D:(i + 1) * D], lhs[:, k, toks(j, i)], w[:, k, :],
                                  start=(k == 0), stop=(k == KD - 1))
                last.then_inc(pe[stage], 1)

            def xT(j):
                transposes("xT", j, xn, (s_n[0], j + 1))

            def gT(j):
                eng.wait_ge(act_m, 1)
                feature_product("gT", j, m1, featA, (cp["xT"], j + 1))

            def v(j):
                token_product("v", j, featA, wsm[:, W_V1], (cp["xT"], j + 1))

            def e1(j):
                eng.wait_ge(cp["gT"], j + 1)
                ps = take_bank(eng, "e1", j)
                for i in range(2):
                    for k in range(KD):
                        last = mm(ps[0:T, i * T:(i + 1) * T], featB[:, k, toks(j, i)], featA[:, k, toks(j, i)],
                                  start=(k == 0), stop=(k == KD - 1))
                last.then_inc(pe["e1"], 1)

            def len1(j):
                eng.wait_ge(s_cnt[0], j + 1)
                mm(bank("e1", j)[0:T, 400:402], cst[0:1, C_ONES:C_ONES + T], cnt[0:1, 0, 2 * j:2 * j + 2],
                   start=True, stop=True).then_inc(pe["len1"], 1)

            def p1T_(j):
                eng.wait_ge(s_exp[0], 2 * j + 2)
                ps = take_bank(eng, "p1T", j)
                for i in range(2):
                    last = nc.tensor.transpose(ps[0:T, i * T:(i + 1) * T], p1[:, 2 * j + i, :], ident[0:T, 0:T])
                last.then_inc(pe["p1T"], 1)

            def z1(j):
                eng.wait_ge(cp["p1T"], j + 1)
                eng.wait_ge(cp["v"], j + 1)
                ps = take_bank(eng, "z1", j)
                for i in range(2):
                    last = mm(ps[0:T, i * D:(i + 1) * D], p1T[:, 2 * j + i, :], vbuf[:, 2 * j + i, :],
                              start=True, stop=True)
                last.then_inc(pe["z1"], 1)

            def x1T(j):
                transposes("x1T", j, rn[:, 1], (s_n[1], j + 1))

            def g2T(j):
                feature_product("g2T", j, m2, featA, (cp["x1T"], 2 * j + 2))

            def e2(j):
                eng.wait_ge(cp["g2T"], j + 1)
                eng.wait_ge(d_ck[j], 32)
                for i in range(2):
                    ps = take_bank(eng, "e2", j, i)
                    for k in range(KD):
                        last = mm(ps[0:T, 0:S], featB[:, k, toks(j, i)], ctxf[:, (2 * j + i) % CR, k, :],
                                  start=(k == 0), stop=(k == KD - 1))
                    last.then_inc(pe["e2"], 1)

            def len2(j):
                for i in range(2):
                    b = 2 * j + i
                    eng.wait_ge(s_cnt[1], b + 1)
                    mm(bank("e2", j, i)[0:T, 400:401], cst[0:1, C_ONES:C_ONES + T], cnt[0:1, 1, b:b + 1],
                       start=True, stop=True).then_inc(pe["len2"], 1)

            def p2T_(j):
                for i in range(2):
                    b = 2 * j + i
                    eng.wait_ge(s_exp[1], b + 1)
                    ps = take_bank(eng, "p2T", j, i)
                    for c in range(KS):
                        last = nc.tensor.transpose(ps[:, c * T:(c + 1) * T], p2[:, b % 4, c * P:(c + 1) * P],
                                                   ident[0:T, 0:T])
                    last.then_inc(pe["p2T"], 1)

            def uT_(j):
                ps = take_bank(eng, "uT", j)
                for i in range(2):
                    b = 2 * j + i
                    eng.wait_ge(cp["p2T"], b + 1)
                    for m in range(KD):
                        for c in range(KS):
                            last = mm(ps[:, (2 * m + i) * T:(2 * m + i + 1) * T],
                                      ctxk[:, b % CR, c, m * P:(m + 1) * P], p2T[:, b % 4, c, :],
                                      start=(c == 0), stop=(c == KS - 1))
                last.then_inc(pe["uT"], 1)

            def z2(j):
                token_product("z2", j, uT, wsm[:, W_V2], (cp["uT"], j + 1))

            def x2T(j):
                transposes("x2T", j, rn[:, 1], (s_n[2], j + 1))

            def f1(j):
                feature_product("f1", j, wsm[:, W_FC1], featA, (cp["x2T"], 2 * j + 2))

            def f2(j):
                token_product("f2", j, featB, wsm[:, W_FC2], (cp["f1"], 2 * j + 2))

            def hT(j):
                transposes("hT", j, xn, (s_n[4], j + 1))

            def route(j):
                if j < PAIRS - 1:
                    return
                eng.wait_ge(cp["hT"], PAIRS)
                eng.wait_ge(d_gate, 16)
                ps = take_bank(eng, "lg", 0)
                for b in range(B):
                    for k in range(KD):
                        last = mm(ps[0:T, b * E:(b + 1) * E], featA[:, k, b * T:(b + 1) * T], gate_sb[:, k, :],
                                  start=(k == 0), stop=(k == KD - 1))
                last.then_inc(pe["lg"], 1)

            def sh(j):
                eng.wait_ge(cp["hT"], j + 1)
                eng.wait_ge(d_sh, 16)
                for q in range(KF // 2):
                    for which, s_ in ((0, "shG"), (1, "shU")):
                        ps = take_bank(eng, "sh", j, 2 * q + which)
                        for fi in range(2):
                            f = 2 * q + fi
                            for k in range(KD):
                                w0 = which * KD * F + k * F + f * P
                                last = mm(ps[:, 2 * fi * T:2 * (fi + 1) * T], wshared[:, w0:w0 + P],
                                          featA[:, k, pair_cols(j)], start=(k == 0), stop=(k == KD - 1))
                        last.then_inc(pe[s_], 1)

            eng.wait_ge(d_w, 16)
            for a, (q, k_, m) in enumerate(((W_Q1T, W_K1T, m1), (W_Q2T, W_K2T, m2))):
                if a == 1:
                    eng.wait_ge(d_w, 32)
                ps = psum[:, BANKS - 1 if a else 0, :]
                for mo in range(KD):
                    for k in range(KD):
                        last = mm(ps[:, mo * D:(mo + 1) * D], wsm[:, q, k, mo * P:(mo + 1) * P], wsm[:, k_, k, :],
                                  start=(k == 0), stop=(k == KD - 1))
                last.then_inc(pe_m, 1)
                if a == 0:
                    eng.wait_ge(d_cst, 16)
            eng.wait_ge(act_m, 2)

            do = dict(xT=xT, gT=gT, v=v, e1=e1, len1=len1, p1T=p1T_, z1=z1, x1T=x1T, g2T=g2T, e2=e2, len2=len2,
                      p2T=p2T_, uT=uT_, z2=z2, x2T=x2T, f1=f1, f2=f2, hT=hT, route=route, sh=sh)
            for s_, j in ORDER:
                if s_ in do:
                    do[s_](j)

            eng.wait_ge(s_lsh, 1)
            eng.wait_ge(s_hs, 2 * PAIRS)

            eng.wait_ge(s_score, 1)
            nc.tensor.transpose(dbank(0)[:, 0:T], score[:].rearrange("t b e -> t (b e)"),
                                ident[0:T, 0:T]).then_inc(pe["sc"], 1)

            def shared_down(j):
                if j >= 2:
                    eng.wait_ge(s_y, j - 1)
                ps = obank(j)
                for i in range(2):
                    for f in range(KF):
                        w0 = 2 * KD * F + f * D
                        last = mm(ps[0:T, i * D:(i + 1) * D], hs[:, f, toks(j, i)], wshared[:, w0:w0 + D],
                                  start=(f == 0), stop=(f == KF - 1))
                last.then_inc(pe["shD"], 1)

            for j in range(PAIRS):
                shared_down(j)

            eng.wait_ge(s_dd, 1)
            eng.wait_ge(s_const, 1)
            for j in range(PAIRS):
                for i in range(2):
                    last = mm(psum[0:T, j, i * EC:(i + 1) * EC], bsel[:, 2 * j + i, :],
                              dix[:].rearrange("p e c -> p (e c)"), start=True, stop=True)
                last.then_inc(pe["bc"], 1)
            eng.wait_ge(s_dd, 2)
            eng.wait_ge(s_S, 1)
            for hf in range(2):
                lo = hf * HALF * CAP
                hi = lo + HALF * CAP
                mm(dbank(0)[0:HALF * CAP, 16 * hf:16 * hf + B], dix[:].rearrange("p e c -> p (e c)")[:, lo:hi],
                   bcol[:], start=True, stop=True)
                last = mm(dbank(0)[0:HALF * CAP, 16 * hf + B:16 * hf + 2 * B],
                          dw[:].rearrange("p e c -> p (e c)")[:, lo:hi], cst[:, C_BATCH:C_BATCH + B],
                          start=True, stop=True)
            last.then_inc(pe["col"], 1)

            GB = [4, 5, 7]
            eng.wait_ge(s_y, PAIRS)
            for b in range(B):
                eng.wait_ge(s_sel, b // 2 + 1)
                if b >= len(GB):
                    eng.wait_ge(s_xg, b - len(GB) + 1)
                ps = psum[:, GB[b % len(GB)], :]
                for m in range(KD):
                    last = mm(ps[:, m * EC:(m + 1) * EC], xn[:, b, m * P:(m + 1) * P], sel[:, b, :],
                              start=True, stop=True)
                last.then_inc(pe["gather"], 1)
            eng.wait_ge(s_xg, B)

            def expert_up(e):
                eng.wait_ge(d_we[e % RING], 16 * (e // RING + 1))
                for which, s_, ps in ((0, "G", gbank(e)), (1, "U", ubank(e))):
                    if e >= 2:
                        eng.wait_ge(s_egel if which == 0 else s_eh, e - 1)
                    for f in range(KF):
                        for k in range(KD):
                            w0 = which * KD * F + k * F + f * P
                            last = mm(ps[:, f * SLOTS:(f + 1) * SLOTS], we[:, e % RING, w0:w0 + P], xg[:, k, e, :],
                                      start=(k == 0), stop=(k == KD - 1))
                    last.then_inc(pe[s_], 1)

            def expert_down(e):
                eng.wait_ge(s_eh, e + 1)
                if e >= 2:
                    eng.wait_ge(s_eo, e - 1)
                for f in range(KF):
                    w0 = 2 * KD * F + f * D
                    last = mm(obank(e)[0:SLOTS, 0:D], hE[:, e % 2, f * SLOTS:(f + 1) * SLOTS],
                              we[:, e % RING, w0:w0 + D], start=(f == 0), stop=(f == KF - 1))
                last.then_inc(pe["eo"], 1)

            def scatter(hf, j):
                if hf == 0 and j >= 2:
                    eng.wait_ge(s_y, PAIRS + j - 1)
                if hf == 1 and j < 2:
                    eng.wait_ge(s_y, PAIRS + j + 3)
                if hf == 1 and j >= 2:
                    eng.wait_ge(s_fin, j - 1)
                n = hf * PAIRS + j
                ps = dbank(n)
                for i in range(2):
                    b = 2 * j + i
                    last = mm(ps[0:T, i * D:(i + 1) * D], wsel[:, hf, b, :], eo_all[:, hf, b, :],
                              start=True, stop=True)
                last.then_inc(pe["scat"], 1)

            for e in range(E + 1):
                if e < E:
                    expert_up(e)
                if e >= 1:
                    expert_down(e - 1)
                if e == HALF + 2:
                    eng.wait_ge(s_wsel, 1)
                    for r in range(2):
                        eng.wait_ge(d_eo[r], 16 * B * (HALF // 2))
                    for j in range(PAIRS):
                        scatter(0, j)
            for r in range(2):
                eng.wait_ge(d_eo[r], 16 * B * HALF)
            for j in range(PAIRS):
                scatter(1, j)

        @block.scalar
        def _(eng):
            act = nc.scalar.activation

            def pairT(ap):
                return ap.rearrange("p (k t) -> p k t", k=KD)

            eng.wait_ge(pe_m, 1)
            nc.scalar.copy(m1.rearrange("p k d -> p (k d)"), psum[:, 0, :]).then_inc(act_m, 1)
            eng.wait_ge(pe_m, 2)
            nc.scalar.copy(m2.rearrange("p k d -> p (k d)"), psum[:, BANKS - 1, :]).then_inc(act_m, 1)

            def copy_pair(stage, dst):
                def f(j):
                    eng.wait_ge(pe[stage], j + 1)
                    nc.scalar.copy(dst[:, :, pair_cols(j)], pairT(bank(stage, j)[:, 0:4 * T])).then_inc(cp[stage], 1)
                return f

            def affine_pair(stage, dst, func, bias, scale):
                def f(j):
                    eng.wait_ge(pe[stage], j + 1)
                    for k in range(KD):
                        act(dst[:, k, pair_cols(j)], bank(stage, j)[:, 2 * k * T:2 * (k + 1) * T], func,
                            bias=cst[:, bias + k:bias + k + 1],
                            scale=cst[:, scale + k:scale + k + 1] if scale else 1.0).then_inc(cp[stage], 1)
                return f

            def soft1(j):
                for i in range(2):
                    b = 2 * j + i
                    eng.wait_ge(s_mask[0], j + 1)
                    act(p1[:, b, :], emk[:, i, 0:T], ACT.Exp, bias=nmax[:, 0, b:b + 1], scale=-1.0,
                        accum_out=rsum[:, 0, b:b + 1]).then_inc(s_exp[0], 1)

            def p1T_(j):
                eng.wait_ge(pe["p1T"], j + 1)
                nc.scalar.copy(p1T[:, 2 * j:2 * j + 2, :],
                               bank("p1T", j)[0:T, 0:2 * T].rearrange("p (i t) -> p i t", i=2)).then_inc(cp["p1T"], 1)

            def v(j):
                eng.wait_ge(pe["v"], j + 1)
                nc.scalar.copy(vbuf[:, 2 * j:2 * j + 2, :],
                               bank("v", j)[0:T, :].rearrange("p (i d) -> p i d", i=2)).then_inc(cp["v"], 1)

            def soft2(j):
                for i in range(2):
                    b = 2 * j + i
                    eng.wait_ge(s_mask[1], b + 1)
                    if b == 0:
                        eng.wait_ge(s_const, 1)
                    if b >= 4:
                        eng.wait_ge(pe["p2T"], b - 3)
                    act(p2[:, b % 4, 0:S], emk[:, i, :], ACT.Exp, bias=nmax[:, 1, b:b + 1], scale=-1.0,
                        accum_out=rsum[:, 1, b:b + 1]).then_inc(s_exp[1], 1)

            def p2T_(j):
                for i in range(2):
                    b = 2 * j + i
                    eng.wait_ge(pe["p2T"], b + 1)
                    if b >= 4:
                        eng.wait_ge(pe["uT"], (b - 4) // 2 + 1)
                    nc.scalar.copy(p2T[:, b % 4],
                                   bank("p2T", j, i)[:, 0:KS * T].rearrange("p (c t) -> p c t", c=KS)
                                   ).then_inc(cp["p2T"], 1)

            def route(j):
                if j == PAIRS - 1:
                    eng.wait_ge(s_lsh, 1)
                    act(lex[:], lsh[:], ACT.Exp).then_inc(s_lex, 1)

            def sh(j):
                for q in range(KF // 2):
                    n = 2 * j + q
                    eng.wait_ge(pe["shG"], n + 1)
                    if n >= 2:
                        eng.wait_ge(s_hs, n - 1)
                    act(gel[:, n % 2, 0:4 * T], bank("sh", j, 2 * q)[:, 0:4 * T], ACT.Gelu).then_inc(s_gel, 1)

            do = dict(xT=copy_pair("xT", featA), gT=copy_pair("gT", featB), v=v, soft1=soft1, p1T=p1T_,
                      x1T=affine_pair("x1T", featA, ACT.Identity, V_B1, V_G1), g2T=copy_pair("g2T", featB),
                      soft2=soft2, p2T=p2T_, uT=copy_pair("uT", uT),
                      x2T=affine_pair("x2T", featA, ACT.Identity, V_B2, V_G2),
                      f1=affine_pair("f1", featB, ACT.Relu, V_FC1, None), hT=copy_pair("hT", featA),
                      route=route, sh=sh)
            for s_, j in ORDER:
                if s_ in do:
                    do[s_](j)

            def eo_copy(e):
                eng.wait_ge(pe["eo"], e + 1)
                if e >= 2:
                    eng.wait_ge(d_eo[e % 2], 16 * B * (e // 2))
                nc.scalar.copy(eo[:, e % 2, :], obank(e)[0:SLOTS, 0:D]).then_inc(s_eo, 1)

            for e in range(E):
                eng.wait_ge(pe["G"], e + 1)
                if e >= 2:
                    eng.wait_ge(s_eh, e - 1)
                else:
                    eng.wait_ge(s_hs, 2 * PAIRS)
                act(gel[:, e % 2, 0:KF * SLOTS], gbank(e)[:, 0:KF * SLOTS], ACT.Gelu).then_inc(s_egel, 1)
                if e >= 1:
                    eo_copy(e - 1)
            eo_copy(E - 1)

        @block.vector
        def _(eng):
            v_ = nc.vector
            chain = [0]

            def then(ins):
                chain[0] += 1
                ins.then_inc(k_dve, 1)
                eng.wait_ge(k_dve, chain[0])

            def stats(n, j, src):
                for i in range(2):
                    last = v_.bn_stats(st6[:, n, 2 * j + i, :], src[:, 2 * j + i, :])
                then(last)
                for i in range(2):
                    last = v_.bn_aggr(mv[:, n, 2 * j + i, :], st6[:, n, 2 * j + i, :])
                last.then_inc(s_mv[n], 1)

            def norm(n, j, dst, src):
                eng.wait_ge(s_rs[n], j + 1)
                for i in range(2):
                    b = 2 * j + i
                    last = v_.tensor_scalar(dst[:, b, :], src[:, b, :], mv[:, n, b, 0:1], rstd[:, n, b, :],
                                            ALU.subtract, ALU.mult)
                last.then_inc(s_n[n], 1)

            def ln0(j):
                eng.wait_ge(d_x, 16 * (j + 1))
                stats(0, j, xres)
                norm(0, j, xn, xres)

            def count(a, j, i):
                b = 2 * j + i
                n = (T, S)[a]
                e_ = bank("e1", j)[0:1, i * T:(i + 1) * T] if a == 0 else bank("e2", j, i)[0:1, 0:S]
                return v_.tensor_scalar(nz[0:1, 0:n], e_, 0.0, None, ALU.not_equal, ALU.add,
                                        accum_out=cnt[0:1, a, b:b + 1])

            def mask(a, j, i):
                b = 2 * j + i
                n = (T, S)[a]
                key = cst[0:T, C_CAUSAL:C_CAUSAL + T] if a == 0 else cst[0:T, C_KEY:C_KEY + S]
                bk = bank("e1", j) if a == 0 else bank("e2", j, i)
                e_ = bk[0:T, i * T:(i + 1) * T] if a == 0 else bk[0:T, 0:S]
                ln = bk[0:T, 400 + (i if a == 0 else 0):401 + (i if a == 0 else 0)]
                then(v_.tensor_scalar(pen[:, i, 0:n], key, ln, FAR, ALU.is_ge, ALU.mult))
                then(v_.reciprocal(linv[:, a, b:b + 1], ln))
                if a == 0 and j >= 1:
                    eng.wait_ge(s_exp[0], 2 * j - 1 + i)
                if a == 1 and j >= 1:
                    eng.wait_ge(s_exp[1], 2 * j - 1 + i)
                return v_.tensor_tensor_reduce(emk[:, i, 0:n], e_, pen[:, i, 0:n], -INV_SQRT_DK, 3.0e38, ALU.add,
                                               ALU.min, nmax[:, a, b:b + 1])

            def soft1(j):
                eng.wait_ge(pe["e1"], j + 1)
                then(count(0, j, 0))
                count(0, j, 1).then_inc(s_cnt[0], 1)
                eng.wait_ge(pe["len1"], j + 1)
                cross_emk(0, j)
                mask(0, j, 0)
                mask(0, j, 1).then_inc(s_mask[0], 1)

            def soft2(j):
                for i in range(2):
                    eng.wait_ge(pe["e2"], 2 * j + i + 1)
                    if i:
                        eng.wait_ge(s_cnt[1], 2 * j + 1)
                    count(1, j, i).then_inc(s_cnt[1], 1)
                cross_emk(1, j)
                for i in range(2):
                    eng.wait_ge(pe["len2"], 2 * j + i + 1)
                    mask(1, j, i).then_inc(s_mask[1], 1)

            seen = []

            def cross_emk(a, j):
                for a0, j0 in reversed(seen):
                    if a0 != a:
                        eng.wait_ge(s_exp[a0], 2 * j0 + 2)
                        break
                seen.append((a, j))

            def invert(a, j):
                eng.wait_ge(s_exp[a], 2 * j + 2)
                c = slice(2 * j, 2 * j + 2)
                then(v_.reciprocal(rinv[:, a, c], rsum[:, a, c]))
                then(v_.scalar_tensor_tensor(rinv[:, a, c], linv[:, a, c], 0.0, rinv[:, a, c], ALU.mult, ALU.add))

            def attend(n, j, stage, res):
                a = n - 1
                invert(a, j)
                eng.wait_ge(pe[stage], j + 1)
                for i in range(2):
                    b = 2 * j + i
                    last = v_.scalar_tensor_tensor(rn[:, 0, b, :], bank(stage, j)[0:T, i * D:(i + 1) * D],
                                                   rinv[:, a, b:b + 1], res[:, b, :], ALU.mult, ALU.add)
                last.then_inc(s_r[n], 1)
                eng.wait_ge(s_r[n], j + 1)
                stats(n, j, rn[:, 0])
                norm(n, j, rn[:, 1], rn[:, 0])

            def ln1(j):
                attend(1, j, "z1", xn)

            def ln2(j):
                eng.wait_ge(s_x1, j + 1)
                attend(2, j, "z2", x1)

            def ln3(j):
                eng.wait_ge(pe["f2"], j + 1)
                eng.wait_ge(s_x2, j + 1)
                c = slice(2 * j, 2 * j + 2)
                v_.tensor_tensor(rn[:, 0, c, :], bank("f2", j)[0:T, :].rearrange("p (i d) -> p i d", i=2),
                                 vbuf[:, c, :], ALU.add).then_inc(s_r[3], 1)
                eng.wait_ge(s_r[3], j + 1)
                stats(3, j, rn[:, 0])
                norm(3, j, rn[:, 1], rn[:, 0])

            def ln4(j):
                eng.wait_ge(s_x3, j + 1)
                stats(4, j, xres)
                norm(4, j, xn, xres)

            def sh(j):
                for q in range(KF // 2):
                    n = 2 * j + q
                    eng.wait_ge(s_gel, n + 1)
                    eng.wait_ge(pe["shU"], n + 1)
                    v_.tensor_tensor(hs[:, 2 * q:2 * q + 2, pair_cols(j)],
                                     gel[:, n % 2, 0:4 * T].rearrange("p (f t) -> p f t", f=2),
                                     bank("sh", j, 2 * q + 1)[:, 0:4 * T].rearrange("p (f t) -> p f t", f=2),
                                     ALU.mult).then_inc(s_hs, 1)

            def route(j):
                if j < PAIRS - 1:
                    return
                eng.wait_ge(pe["lg"], 1)
                lg = bank("lg", 0)[0:T, 0:B * E].rearrange("p (b e) -> p b e", b=B)
                then(v_.tensor_reduce(lmx[:], lg, AX.X, ALU.max))
                v_.tensor_tensor(lsh[:], lg, lmx[:].unsqueeze(2).to_broadcast([T, B, E]),
                                 ALU.subtract).then_inc(s_lsh, 1)
                eng.wait_ge(s_lex, 1)
                then(v_.tensor_reduce(lsum[:], lex[:], AX.X, ALU.add))
                then(v_.reciprocal(lri[:], lsum[:]))
                v_.tensor_tensor(score[:], lex[:], lri[:].unsqueeze(2).to_broadcast([T, B, E]),
                                 ALU.mult).then_inc(s_score, 1)

            v_.memset(p2[:, :, S:SP_], 0.0)
            eng.wait_ge(d_cst, 16)
            v_.tensor_copy(bcol[:], cst[:, C_BATCH:C_BATCH + B])
            v_.tensor_copy(bsel[:], cst[:, C_BATCH:C_BATCH + B].unsqueeze(2).to_broadcast([P, B, T])
                           ).then_inc(s_const, 1)

            do = dict(ln0=ln0, soft1=soft1, ln1=ln1, soft2=soft2, ln2=ln2, ln3=ln3, ln4=ln4, route=route, sh=sh)
            for s_, j in ORDER:
                if s_ in do:
                    do[s_](j)

            eng.wait_ge(pe["sc"], 1)
            v_.tensor_copy(sS[:], dbank(0)[:, 0:T]).then_inc(s_S, 1)
            eng.wait_ge(s_S, 1)
            then(v_.max(top[:, 0:8], sS[:]))
            v_.max_index(tix[:, 0:8], top[:, 0:8], sS[:])
            then(v_.match_replace(sS2[:], top[:, 0:8], sS[:], -1.0))
            then(v_.max(top[:, 8:16], sS2[:]))
            then(v_.max_index(tix[:, 8:16], top[:, 8:16], sS2[:]))
            then(v_.tensor_copy(tixf[:], tix[:]))
            em = cst[:, C_EMASK:C_EMASK + E].unsqueeze(2).to_broadcast([P, E, CAP])
            v_.tensor_tensor(dix[:], em, tixf[:, 0:CAP].unsqueeze(1).to_broadcast([P, E, CAP]),
                             ALU.mult).then_inc(s_dd, 1)
            v_.tensor_tensor(dw[:], em, top[:, 0:CAP].unsqueeze(1).to_broadcast([P, E, CAP]),
                             ALU.mult).then_inc(s_dd, 1)

            def add_shared(j):
                eng.wait_ge(pe["shD"], j + 1)
                c = slice(2 * j, 2 * j + 2)
                v_.tensor_tensor(xres[:, c, :], obank(j)[0:T, :].rearrange("p (i d) -> p i d", i=2),
                                 xres[:, c, :], ALU.add).then_inc(s_y, 1)

            for j in range(PAIRS):
                add_shared(j)
            for j in range(PAIRS):
                eng.wait_ge(pe["bc"], j + 1)
                v_.tensor_scalar(sel[:, 2 * j:2 * j + 2, :],
                                 psum[0:T, j, 0:2 * EC].rearrange("p (i c) -> p i c", i=2),
                                 cst[0:T, C_ROW:C_ROW + 1], None, ALU.is_equal).then_inc(s_sel, 1)
            eng.wait_ge(pe["col"], 1)
            v_.tensor_copy(wcol[:].rearrange("p h a b -> p (h a b)"),
                           dbank(0)[0:HALF * CAP, 0:32]).then_inc(s_col, 1)
            for b in range(B):
                eng.wait_ge(pe["gather"], b + 1)
                for m in range(KD):
                    last = v_.tensor_copy(
                        xg[:, m, :, b * CAP:(b + 1) * CAP],
                        psum[:, [4, 5, 7][b % 3], m * EC:(m + 1) * EC].rearrange("p (e c) -> p e c", e=E))
                last.then_inc(s_xg, 1)
            eng.wait_ge(s_col, 1)
            for hf in range(2):
                for b in range(B):
                    last = v_.tensor_scalar(wsel[:, hf, b, :], cst[0:HALF * CAP, C_KEY:C_KEY + T],
                                            wcol[:, hf, 0, b:b + 1], wcol[:, hf, 1, b:b + 1],
                                            ALU.is_equal, ALU.mult)
            last.then_inc(s_wsel, 1)

            def add_scatter(hf, j):
                eng.wait_ge(pe["scat"], hf * PAIRS + j + 1)
                if hf == 0:
                    eng.wait_ge(s_y, j + 1)
                else:
                    eng.wait_ge(s_y, PAIRS + j + 1)
                c = slice(2 * j, 2 * j + 2)
                v_.tensor_tensor(xres[:, c, :], dbank(hf * PAIRS + j)[0:T, :].rearrange("p (i d) -> p i d", i=2),
                                 xres[:, c, :], ALU.add).then_inc(s_fin if hf else s_y, 1)

            for e in range(E):
                eng.wait_ge(s_egel, e + 1)
                eng.wait_ge(pe["U"], e + 1)
                if e >= 2:
                    eng.wait_ge(pe["eo"], e - 1)
                v_.tensor_tensor(hE[:, e % 2, :], gel[:, e % 2, 0:KF * SLOTS], ubank(e)[:, 0:KF * SLOTS],
                                 ALU.mult).then_inc(s_eh, 1)
                if e == HALF + 2:
                    for j in range(PAIRS):
                        add_scatter(0, j)
            for j in range(PAIRS):
                add_scatter(1, j)

        @block.gpsimd
        def _(eng):
            g_ = nc.gpsimd
            chain = [0]

            def then(ins):
                chain[0] += 1
                ins.then_inc(k_pool, 1)
                eng.wait_ge(k_pool, chain[0])

            def rs(n):
                def f(j):
                    c = slice(2 * j, 2 * j + 2)
                    eng.wait_ge(s_mv[n], j + 1)
                    then(g_.tensor_scalar_add(ve[:, n, c, :], mv[:, n, c, 1:2], EPS))
                    g_.tensor_tensor(rstd[:, n, c, :], ve[:, n, c, :], nhalf[:], ALU.pow).then_inc(s_rs[n], 1)
                return f

            def affine(dst, src, g, b, done):
                then(g_.tensor_tensor(dst, src, bcast_row(g), ALU.mult))
                g_.tensor_tensor(dst, dst, bcast_row(b), ALU.add).then_inc(done, 1)

            def ln0(j):
                rs(0)(j)

            def ln1(j):
                rs(1)(j)
                eng.wait_ge(s_n[1], j + 1)
                c = slice(2 * j, 2 * j + 2)
                affine(x1[:, c, :], rn[:, 1, c, :], R_G1, R_B1, s_x1)

            def xb(j):
                eng.wait_ge(s_n[0], j + 1)
                c = slice(2 * j, 2 * j + 2)
                g_.tensor_tensor(xres[:, c, :], xres[:, c, :], bcast_row(R_B3), ALU.add).then_inc(s_xb, 1)

            def ln2(j):
                rs(2)(j)
                eng.wait_ge(s_n[2], j + 1)
                c = slice(2 * j, 2 * j + 2)
                affine(vbuf[:, c, :], rn[:, 1, c, :], R_G2, R_B2, s_x2)

            def ln3(j):
                rs(3)(j)
                eng.wait_ge(s_n[3], j + 1)
                eng.wait_ge(s_xb, j + 1)
                c = slice(2 * j, 2 * j + 2)
                then(g_.tensor_tensor(rn[:, 1, c, :], rn[:, 1, c, :], bcast_row(R_G3), ALU.mult))
                g_.tensor_tensor(xres[:, c, :], xres[:, c, :], rn[:, 1, c, :], ALU.add).then_inc(s_x3, 1)

            def ln4(j):
                rs(4)(j)

            then(g_.memset(nhalf[:], -0.5))
            do = dict(ln0=ln0, ln1=ln1, soft1=xb, ln2=ln2, ln3=ln3, ln4=ln4)
            first = True
            for s_, j in ORDER:
                if s_ == "soft1" and first:
                    eng.wait_ge(d_row, 16)
                    then(g_.tensor_tensor(row[:, R_B2, :], row[:, R_B2, :], row[:, R_FC2, :], ALU.add))
                    first = False
                if s_ in do:
                    do[s_](j)


_NAMES = ("x", "ctx_tok", "ctx_feat", "w_small", "consts", "rows", "gate", "w_moe")


def kernel(**inputs):
    import numpy as _np
    import concourse.bacc as _bacc
    from concourse import mybir as _mybir
    from concourse.bass_utils import run_bass_kernel_spmd as _run

    a = {k: _np.asarray(v) for k, v in inputs.items()}
    f32 = _np.float32

    def chunked(w):
        return w.reshape(-1, P, w.shape[1]).transpose(1, 0, 2)

    def vec(v):
        return v.reshape(KD, P).T

    ctx = a["ctx_1024"]
    ctx_tok = _np.concatenate([ctx, _np.zeros((B, SP_ - S, D), f32)], axis=1)
    ctx_tok = ctx_tok.reshape(B, KS, P, D).transpose(2, 0, 1, 3)
    ctx_feat = ctx.reshape(B, S, KD, P).transpose(3, 0, 2, 1)
    w_small = _np.stack([chunked(w) for w in (
        a["L0_xattn_Wq1"].T, a["L0_xattn_Wk1"].T, a["L0_xattn_Wv1"], a["L0_xattn_Wq2"].T, a["L0_xattn_Wk2"].T,
        a["L0_xattn_Wv2"], a["L0_xattn_fc1_w"], a["L0_xattn_fc2_w"])], axis=1)
    part = _np.arange(P)
    key = _np.arange(S)
    causal = _np.where(key[None, :T] > part[:, None], 4 * S, key[None, :T])
    consts = _np.concatenate([
        _np.eye(P), causal, _np.broadcast_to(key, (P, S)), part[:, None],
        part[:, None] % E == _np.arange(E)[None], part[:, None] // E == _np.arange(B)[None],
        _np.ones((P, T))], axis=1).astype(f32)
    consts = _np.concatenate([consts] + [vec(a["L0_xattn_" + n]) for n in
                                         ("ln1_g", "ln1_b", "ln2_g", "ln2_b", "fc1_b")], axis=1)
    rows = _np.stack([a["L0_xattn_" + n] for n in ("ln1_g", "ln1_b", "ln2_g", "ln2_b", "ln3_g", "ln3_b", "fc2_b")])
    gate = chunked(a["L0_ffn_gate_w"].T)

    def moe(g, u, d):
        return _np.concatenate([chunked(w.T).reshape(P, -1) for w in (g, u, d)], axis=1)

    w_moe = _np.stack([moe(a["L0_ffn_Wg"][e], a["L0_ffn_Wu"][e], a["L0_ffn_Wd"][e]) for e in range(E)]
                      + [moe(a["L0_ffn_Ws_g"], a["L0_ffn_Ws_u"], a["L0_ffn_Ws_d"])])
    data = dict(x=a["x"], ctx_tok=ctx_tok, ctx_feat=ctx_feat, w_small=w_small, consts=consts, rows=rows,
                gate=gate, w_moe=w_moe)

    nc = _bacc.Bacc("TRN2", target_bir_lowering=False, num_devices=1)
    arrays, args = {}, []
    for name in _NAMES:
        arr = _np.ascontiguousarray(data[name])
        arrays[f"in_{name}"] = arr
        args.append(nc.dram_tensor(f"in_{name}", arr.shape, _mybir.dt.from_np(arr.dtype), kind="ExternalInput").ap())
    args.append(nc.dram_tensor("out_0", (B, T, D), F32, kind="ExternalOutput").ap())
    xattn_moe(nc, *args)
    r = _run(nc, [arrays], core_ids=[0])
    return r.results[0]["out_0"]
```

```python
from contextlib import ExitStack

import concourse.bass as bass
from concourse import mybir

ALU = mybir.AluOpType
ACT = mybir.ActivationFunctionType
AX = mybir.AxisListType
F32 = mybir.dt.float32
BF16 = mybir.dt.bfloat16
U32 = mybir.dt.uint32

P = 128
B, T, D = 8, 100, 256
S = 361
NT = B * T
KD = D // P
KS = -(-S // P)
SP_ = KS * P
PAIRS = B // 2
E, F = 16, 512
KF = F // P
CAP = int(T * 2.0 / E)
SLOTS = B * CAP
HALF = E // 2
EC = E * CAP
INV_SQRT_DK = 1.0 / (D // 16) ** 0.5
EPS = 1e-5
FAR = -3.0e38
WE = 2 * KD * F + KF * D
RING = 4
BANKS = 8

C_IDENT = 0
C_CAUSAL = C_IDENT + P
C_KEY = C_CAUSAL + T
C_ROW = C_KEY + S
C_EMASK = C_ROW + 1
C_BATCH = C_EMASK + E
C_ONES = C_BATCH + B
C_VEC = C_ONES + T
C_END = C_VEC + 5 * KD
V_G1, V_B1, V_G2, V_B2, V_FC1 = (C_VEC + KD * i for i in range(5))
R_G1, R_B1, R_G2, R_B2, R_G3, R_B3, R_FC2 = range(7)
W_Q1T, W_K1T, W_V1, W_Q2T, W_K2T, W_V2, W_FC1, W_FC2 = range(8)


PE_, ACT_, DVE_, POOL_, MOVE_ = "PE", "ACT", "DVE", "POOL", "MOVE"
HOP = 0.2


def tasks():
    out = {}

    def add(name, unit, engine, cost, after=(), banks=0, freed_by=None):
        out[(name, unit)] = dict(engine=engine, cost=cost, after=[a for a in after if a is not None], banks=banks,
                                 freed_by=freed_by)

    add("m1", 0, PE_, 1.8, [], 1, [("m1c", 0)])
    add("m1c", 0, ACT_, 0.5, [("m1", 0)])
    add("m2", 0, PE_, 1.8, [("nm0", 1)], 1, [("m2c", 0)])
    add("m2c", 0, ACT_, 0.5, [("m2", 0)])
    for j in range(PAIRS):
        both = (2 * j, 2 * j + 1)

        def norm(n, before):
            add(f"rs{n}", j, POOL_, 0.9, before)
            add(f"nm{n}", j, DVE_, 0.7, [(f"rs{n}", j)])

        def turned(name, src, cost=0.4):
            add(name, j, PE_, 0.4, [src], 1, [(name + "c", j)])
            add(name + "c", j, ACT_, cost, [(name, j)])

        def product(name, cost, after, copy=0.4):
            add(name, j, PE_, cost, after, 1, [(name + "c", j)])
            add(name + "c", j, ACT_, copy, [(name, j)])

        add("st0", j, DVE_, 0.9)
        norm(0, [("st0", j)])
        turned("xT", ("nm0", j))
        product("gT", 1.4, [("xTc", j), ("m1c", 0)])
        product("v", 1.8, [("xTc", j)], 0.5)
        add("e1", j, PE_, 0.9, [("gTc", j)], 1, [("mask1", j)])
        add("cnt1", j, DVE_, 0.45, [("e1", j)])
        add("len1", j, PE_, 0.15, [("cnt1", j)])
        add("mask1", j, DVE_, 0.95, [("len1", j), ("exp1", j - 1) if j else None])
        add("exp1", j, ACT_, 0.75, [("mask1", j)])
        turned("p1T", ("exp1", j), 0.25)
        add("z1", j, PE_, 0.9, [("p1Tc", j), ("vc", j)], 1, [("sum1", j)])
        add("inv1", j, DVE_, 0.25, [("exp1", j)])
        add("sum1", j, DVE_, 1.8, [("z1", j), ("inv1", j)])
        norm(1, [("sum1", j)])
        add("x1a", j, POOL_, 2.6, [("nm1", j)])
        turned("x1T", ("nm1", j), 0.7)
        product("g2T", 1.4, [("x1Tc", j), ("m2c", 0)])
        for b in both:
            add("e2", b, PE_, 1.2, [("g2Tc", j)], 1, [("mask2", b)])
            add("cnt2", b, DVE_, 0.45, [("e2", b)])
            add("len2", b, PE_, 0.1, [("cnt2", b)])
            add("mask2", b, DVE_, 1.0, [("len2", b), ("exp2", b - 2) if b > 1 else None])
            add("exp2", b, ACT_, 0.6, [("mask2", b), ("p2T", b - 4) if b > 3 else None,
                                       ("exp1", PAIRS - 1) if b in (2, 3) else None])
            add("p2T", b, PE_, 0.3, [("exp2", b)], 1, [("p2Tc", b)])
            add("p2Tc", b, ACT_, 0.35, [("p2T", b), ("u", (b - 4) // 2) if b > 3 else None])
        add("inv2", j, DVE_, 0.25, [("exp2", b) for b in both])
        add("u", j, PE_, 2.6, [("p2Tc", b) for b in both], 1, [("uc", j)])
        add("uc", j, ACT_, 0.75, [("u", j), ("inv2", j)])
        turned("uT", ("uc", j))
        add("z2", j, PE_, 1.8, [("uTc", j)], 1, [("sum2", j)])
        add("sum2", j, DVE_, 1.6, [("z2", j), ("x1a", j)])
        norm(2, [("sum2", j)])
        add("x2a", j, POOL_, 2.6, [("nm2", j)])
        turned("x2T", ("nm2", j), 0.7)
        product("f1", 1.4, [("x2Tc", j)], 0.7)
        add("f2", j, PE_, 1.8, [("f1c", j)], 1, [("sum3", j)])
        add("sum3", j, DVE_, 1.6, [("f2", j), ("x2a", j)])
        norm(3, [("sum3", j)])
        add("xb", j, POOL_, 1.3, [("nm0", j)])
        add("x3", j, POOL_, 2.6, [("nm3", j), ("xb", j)])
        add("st4", j, DVE_, 0.9, [("x3", j)])
        norm(4, [("st4", j)])
        turned("hT", ("nm4", j))
        for q in range(2):
            n = 2 * j + q
            add("shG", n, PE_, 1.4, [("hTc", j)], 1, [("gel", n)])
            add("shU", n, PE_, 1.4, [("hTc", j)], 1, [("hs", n)])
            add("gel", n, ACT_, 0.45, [("shG", n), ("hs", n - 2) if n > 1 else None, ("z1", PAIRS - 1)])
            add("hs", n, DVE_, 0.55, [("gel", n), ("shU", n), ("u", 1)])
        add("sd", j, PE_, 3.5, [("hs", 2 * j + 1)], 1, [("y", j)])
        add("y", j, DVE_, 0.65, [("sd", j)])
        add("bc", j, PE_, 0.2, [("dix", 0)], 1, [("sel", j)])
        add("sel", j, DVE_, 0.5, [("bc", j)])
    add("lg", 0, PE_, 3.4, [("hTc", j) for j in range(PAIRS)], 1, [("lsh", 0)])
    add("lsh", 0, DVE_, 0.5, [("lg", 0)])
    add("lex", 0, ACT_, 0.3, [("lsh", 0)])
    add("score", 0, DVE_, 0.7, [("lex", 0)])
    add("scT", 0, PE_, 0.1, [("score", 0)], 1, [("sc", 0)])
    add("sc", 0, DVE_, 0.2, [("scT", 0)])
    add("dix", 0, DVE_, 2.2, [("sc", 0)])
    add("col", 0, PE_, 0.5, [("dix", 0)], 1, [("wcol", 0)])
    add("wcol", 0, DVE_, 0.2, [("col", 0)])
    add("wsel", 0, DVE_, 2.5, [("wcol", 0)])
    for j in range(PAIRS):
        add("ga0", j, PE_, 0.8, [("sel", j)], 1, [("xg0", j)])
        add("xg0", j, DVE_, 0.4, [("ga0", j), ("u", 1)])
        add("ga1", j, PE_, 0.8, [("sel", j)], 1, [("xg1", j)])
        add("xg1", j, ACT_, 0.4, [("ga1", j), ("u", 1)])
    for e in range(E):
        start = [("xg0", PAIRS - 1), ("xg1", PAIRS - 1)]
        add("G", e, PE_, 1.7, start, 1, [("gelE", e)])
        add("U", e, PE_, 1.7, start, 1, [("hE", e)])
        add("gelE", e, ACT_, 0.4, [("G", e), ("hE", e - 2) if e > 1 else None, ("hs", 2 * PAIRS - 1)])
        add("hE", e, DVE_, 0.45, [("gelE", e), ("U", e), ("D", e - 2) if e > 1 else None])
        add("D", e, PE_, 1.7, [("hE", e)], 1, [("eo", e)])
        add("eo", e, ACT_, 0.35, [("D", e), ("mv", e - 2) if e > 1 else None])
        add("mv", e, MOVE_, 2.6, [("eo", e)])
    for hf in range(2):
        for j in range(PAIRS):
            n = hf * PAIRS + j
            add("scat", n, PE_, 0.9, [("mv", hf * HALF + HALF - 1), ("wsel", 0)], 1, [("fin", n)])
            add("fin", n, DVE_, 0.65, [("scat", n), ("y", j)])
    for name, unit in list(out):
        if (name, unit - 1) in out:
            out[(name, unit)]["after"].append((name, unit - 1))
    return out


def plan():
    todo = tasks()
    behind = {}

    def work_behind(t):
        if t not in behind:
            behind[t] = todo[t]["cost"] + HOP + max([work_behind(u) for u in later[t]], default=0.0)
        return behind[t]

    later = {t: [] for t in todo}
    for t, x in todo.items():
        for a in x["after"]:
            later[a].append(t)
    free = {e: 0.0 for e in (PE_, ACT_, DVE_, POOL_, MOVE_)}
    ended, order, banks = {}, [], {}
    bank_user = [None] * BANKS
    left = set(todo)
    while left:
        best = None
        for t in left:
            x = todo[t]
            if any(a not in ended for a in x["after"]):
                continue
            at = free[x["engine"]]
            for a in x["after"]:
                at = max(at, ended[a] + (0.0 if todo[a]["engine"] == x["engine"] else HOP))
            if x["banks"]:
                gone = [0.0 if u is None else max((ended.get(f, 1e9) for f in todo[u]["freed_by"])) + HOP
                        for u in bank_user]
                at = max(at, min(gone))
                if at > 1e8:
                    continue
            key = (round(at, 3), -work_behind(t), t)
            if best is None or key < best[0]:
                best = (key, t, at)
        _, t, at = best
        x = todo[t]
        if x["banks"]:
            ready = [(0.0 if u is None else max((ended.get(f, 1e9) for f in todo[u]["freed_by"])) + HOP, n)
                     for n, u in enumerate(bank_user)]
            n = min(ready)[1]
            banks[t] = (n, bank_user[n])
            bank_user[n] = t
        ended[t] = at + x["cost"]
        free[x["engine"]] = ended[t]
        order.append(t)
        left.remove(t)
    return order, banks, {t: x["freed_by"] for t, x in todo.items() if x["banks"]}


def xattn_moe(nc, x, ctx_tok, ctx_feat, w_small, consts, rows, gate, w_moe, out):
    stack = ExitStack()
    with stack:
        def sb(name, shape, dt=F32):
            return stack.enter_context(nc.sbuf_tensor(name, shape, dt))

        def sem(name):
            return stack.enter_context(nc.semaphore(name))

        cst = sb("cst", [P, C_END])
        row = sb("row", [P, 7, D])
        wsm = sb("wsm", [P, 8, KD, D])
        m1 = wsm[:, W_Q1T]
        m2 = wsm[:, W_Q2T]
        gate_sb = sb("gate_sb", [P, KD, E])
        xres = sb("xres", [T, B, D])
        xn = sb("xn", [T, B, D])
        featA = sb("featA", [P, KD, NT])
        featB = sb("featB", [P, KD, NT])
        vbuf = sb("vbuf", [T, B, D])
        rn = sb("rn", [T, 2, B, D])
        x1 = sb("x1", [T, B, D])
        masks = sb("masks", [P, 2, 2, S])
        pen = masks[0:T, 0]
        emk = masks[0:T, 1]
        probs = sb("probs", [P, 2, B, T])
        p1 = probs[0:T, 0]
        p1T = probs[0:T, 1]
        cross = sb("cross", [P, 4, SP_])
        p2 = cross[0:T]
        pen1 = cross[0:T, 2, 0:2 * T].rearrange("p (i t) -> p i t", i=2)
        emk1 = cross[0:T, 3, 0:2 * T].rearrange("p (i t) -> p i t", i=2)
        p2T = sb("p2T", [P, 4, KS, T])
        uT = sb("uT", [P, KD, NT])
        u = rn[:, 0]
        we = sb("we", [P, RING, WE])
        region = sb("region", [P, 2 * WE + 128])

        def context(j):
            place = region[:, j * WE:(j + 1) * WE] if j < 2 else we[:, j, :]
            n = 2 * KS * D
            return (place[:, 0:n].rearrange("p (b c d) -> p b c d", b=2, c=KS),
                    place[:, n:n + 2 * KD * S].rearrange("p (b k s) -> p b k s", b=2, k=KD))

        wshared = sb("wshared", [P, WE])
        st6 = sb("st6", [T, 5, B, 6])
        mv = sb("mv", [T, 5, B, 2])
        ve = sb("ve", [T, 5, B, 1])
        rstd = sb("rstd", [T, 5, B, 1])
        nhalf = sb("nhalf", [T, 2, 1])
        nz = sb("nz", [1, S])
        cnt = sb("cnt", [1, 2, B])
        nmax = sb("nmax", [T, 2, B])
        rsum = sb("rsum", [T, 2, B])
        rinv = sb("rinv", [T, 2, B])
        linv = sb("linv", [T, 2, B])
        hs = region[:, 0:KF * NT].rearrange("p (f t) -> p f t", f=KF)
        xg = region[:, KF * NT:KF * NT + KD * E * SLOTS].rearrange("p (k e s) -> p k e s", k=KD, e=E)
        eo_all = rn[0:HALF * CAP]
        sel = vbuf[:].rearrange("t b d -> t (b d)")[:, 0:B * EC].rearrange("t (b c) -> t b c", b=B)
        wsel = x1[:].rearrange("t b d -> t (b d)")[0:HALF * CAP, 0:2 * B * T].rearrange(
            "p (h b t) -> p h b t", h=2, b=B)
        late = probs[:].rearrange("p a b t -> p (a b t)")
        gel = late[:, 0:2 * 4 * T].rearrange("p (r c) -> p r c", r=2)
        eo = late[0:SLOTS, 2 * 4 * T:2 * 4 * T + 2 * D].rearrange("p (r d) -> p r d", r=2)
        hE = masks[:].rearrange("p a b s -> p (a b s)")[:, 0:2 * KF * SLOTS].rearrange("p (r c) -> p r c", r=2)
        lmx = sb("lmx", [T, B])
        gate_rows = vbuf[:].rearrange("t b d -> t (b d)")[:, B * EC:B * EC + 3 * B * E].rearrange(
            "t (a b e) -> t a b e", a=3, b=B)
        lsh = gate_rows[:, 0]
        lex = gate_rows[:, 1]
        score = gate_rows[:, 2]
        lsum = sb("lsum", [T, B])
        lri = sb("lri", [T, B])
        sS = sb("sS", [P, T])
        sS2 = sb("sS2", [P, T])
        top = sb("top", [P, 16])
        tix = sb("tix", [P, 16], U32)
        tixf = sb("tixf", [P, 16])
        dix = sb("dix", [P, E, CAP], BF16)
        dw = cross[:, 0, 0:EC].rearrange("p (e c) -> p e c", e=E)
        bsel = sb("bsel", [P, B, T], BF16)
        bcol = sb("bcol", [P, B], BF16)
        wcol = sb("wcol", [HALF * CAP, 2, 2, B])

        psum = stack.enter_context(nc.psum_tensor("psum", [P, BANKS, 512], F32))

        ident = cst[:, C_IDENT:C_IDENT + P]

        d_x = [sem(f"d_x{j}") for j in range(PAIRS)]
        d_cst, d_w1, d_w2, d_row, d_gate, d_sh, d_out = (
            sem(n) for n in ("d_cst", "d_w1", "d_w2", "d_row", "d_gate", "d_sh", "d_out"))
        d_ck = [sem(f"d_ck{j}") for j in range(PAIRS)]
        d_we = [sem(f"d_we{i}") for i in range(RING)]
        d_mv = [sem(f"d_mv{i}") for i in range(2)]
        s_const, s_b2 = sem("s_const"), sem("s_b2")
        k_dve, k_pool = sem("k_dve"), sem("k_pool")

        ORDER, BANK, FREED_BY = plan()
        done = {name: sem("done_" + name) for name in dict.fromkeys(name for name, _ in ORDER) if name != "mv"}

        def bank(name, unit):
            return psum[:, BANK[(name, unit)][0], :]

        def take_bank(eng, name, unit):
            before = BANK[(name, unit)][1]
            if before is not None:
                for reader, u_ in FREED_BY[before]:
                    eng.wait_ge(done[reader], u_ + 1)
            return bank(name, unit)

        def toks(b):
            return slice(b * T, (b + 1) * T)

        def pair_cols(j):
            return slice(2 * j * T, (2 * j + 2) * T)

        def pair(j):
            return slice(2 * j, 2 * j + 2)

        def bcast_row(r):
            return row[0:T, r, :].unsqueeze(1).to_broadcast([T, 2, D])

        block = stack.enter_context(nc.Block())

        @block.sync
        def _(sp):
            xv = x.rearrange("b t d -> t b d")

            def load_ctx(j):
                ctxk, ctxf = context(j)
                sp.dma_start(ctxf, ctx_feat[:, pair(j)]).then_inc(d_ck[j], 16)
                sp.dma_start(ctxk, ctx_tok[:, pair(j)]).then_inc(d_ck[j], 16)

            def load_expert(e):
                if e >= RING:
                    sp.wait_ge(done["D"], e - RING + 1)
                elif e >= 2:
                    sp.wait_ge(done["u"], e + 1)
                    sp.wait_ge(done["e2"], 2 * e + 2)
                sp.dma_start(we[:, e % RING], w_moe[e]).then_inc(d_we[e % RING], 16)

            sp.dma_start(xres[:, pair(0), :], xv[:, pair(0), :]).then_inc(d_x[0], 16)
            sp.dma_start(wsm[:, 0:2], w_small[:, 0:2]).then_inc(d_w1, 16)
            sp.dma_start(cst[:], consts).then_inc(d_cst, 16)
            sp.dma_start(xres[:, pair(1), :], xv[:, pair(1), :]).then_inc(d_x[1], 16)
            sp.dma_start(wsm[:, 2:8], w_small[:, 2:8]).then_inc(d_w2, 16)
            for j in range(2, PAIRS):
                sp.dma_start(xres[:, pair(j), :], xv[:, pair(j), :]).then_inc(d_x[j], 16)
            sp.dma_start(row[:], rows.partition_broadcast(P)).then_inc(d_row, 16)
            for j in range(PAIRS):
                load_ctx(j)
            sp.dma_start(gate_sb[:], gate).then_inc(d_gate, 16)
            sp.dma_start(wshared[:], w_moe[E]).then_inc(d_sh, 16)
            for e in range(RING):
                load_expert(e)

            for e in range(E):
                sp.wait_ge(done["eo"], e + 1)
                r0 = (e % HALF) * CAP
                sp.dma_start(eo_all[r0:r0 + CAP, e // HALF], eo[:, e % 2, :]).then_inc(d_mv[e % 2], 16)
                if e + RING < E:
                    load_expert(e + RING)

            ov = out.rearrange("b t d -> t b d")
            for j in range(PAIRS):
                sp.wait_ge(done["fin"], PAIRS + j + 1)
                sp.dma_start(ov[:, pair(j), :], xres[:, pair(j), :]).then_inc(d_out, 16)
            sp.wait_ge(d_out, 16 * PAIRS)

        @block.tensor
        def _(eng):
            mm = nc.tensor.matmul

            def fused_weights(name, wq, wk, loaded):
                def f(_):
                    eng.wait_ge(loaded, 16)
                    ps = take_bank(eng, name, 0)
                    for m in range(KD):
                        for k in range(KD):
                            last = mm(ps[:, m * D:(m + 1) * D], wsm[:, wq, k, m * P:(m + 1) * P], wsm[:, wk, k, :],
                                      start=(k == 0), stop=(k == KD - 1))
                    last.then_inc(done[name], 1)
                return f

            def turn(name, src, ready):
                def f(j):
                    eng.wait_ge(done[ready], j + 1)
                    if name == "xT" and j == 0:
                        eng.wait_ge(d_cst, 16)
                    ps = take_bank(eng, name, j)
                    for k in range(KD):
                        for i in range(2):
                            c0 = (2 * k + i) * T
                            last = nc.tensor.transpose(ps[:, c0:c0 + T], src[:, 2 * j + i, k * P:(k + 1) * P],
                                                       ident[0:T, 0:T])
                    last.then_inc(done[name], 1)
                return f

            def by_feature(name, w, rhs, ready, weights=None):
                def f(j):
                    if weights and j == 0:
                        eng.wait_ge(*weights)
                    eng.wait_ge(done[ready], j + 1)
                    ps = take_bank(eng, name, j)
                    for m in range(KD):
                        for k in range(KD):
                            last = mm(ps[:, 2 * m * T:2 * (m + 1) * T], w[:, k, m * P:(m + 1) * P],
                                      rhs[:, k, pair_cols(j)], start=(k == 0), stop=(k == KD - 1))
                    last.then_inc(done[name], 1)
                return f

            def by_token(name, lhs, w, ready):
                def f(j):
                    if j == 0:
                        eng.wait_ge(d_w2, 16)
                    eng.wait_ge(done[ready], j + 1)
                    ps = take_bank(eng, name, j)
                    for i in range(2):
                        for k in range(KD):
                            last = mm(ps[0:T, i * D:(i + 1) * D], lhs[:, k, toks(2 * j + i)], w[:, k, :],
                                      start=(k == 0), stop=(k == KD - 1))
                    last.then_inc(done[name], 1)
                return f

            def e1(j):
                eng.wait_ge(done["gTc"], j + 1)
                ps = take_bank(eng, "e1", j)
                for i in range(2):
                    b = 2 * j + i
                    for k in range(KD):
                        last = mm(ps[0:T, i * T:(i + 1) * T], featB[:, k, toks(b)], featA[:, k, toks(b)],
                                  start=(k == 0), stop=(k == KD - 1))
                last.then_inc(done["e1"], 1)

            def len1(j):
                eng.wait_ge(done["cnt1"], j + 1)
                mm(bank("e1", j)[0:T, 400:402], cst[0:1, C_ONES:C_ONES + T], cnt[0:1, 0, pair(j)],
                   start=True, stop=True).then_inc(done["len1"], 1)

            def p1T_(j):
                eng.wait_ge(done["exp1"], j + 1)
                ps = take_bank(eng, "p1T", j)
                for i in range(2):
                    last = nc.tensor.transpose(ps[0:T, i * T:(i + 1) * T], p1[:, 2 * j + i, :], ident[0:T, 0:T])
                last.then_inc(done["p1T"], 1)

            def z1(j):
                eng.wait_ge(done["p1Tc"], j + 1)
                eng.wait_ge(done["vc"], j + 1)
                ps = take_bank(eng, "z1", j)
                for i in range(2):
                    last = mm(ps[0:T, i * D:(i + 1) * D], p1T[:, 2 * j + i, :], vbuf[:, 2 * j + i, :],
                              start=True, stop=True)
                last.then_inc(done["z1"], 1)

            def e2(b):
                eng.wait_ge(done["g2Tc"], b // 2 + 1)
                eng.wait_ge(d_ck[b // 2], 32)
                ps = take_bank(eng, "e2", b)
                for k in range(KD):
                    last = mm(ps[0:T, 0:S], featB[:, k, toks(b)], context(b // 2)[1][:, b % 2, k, :],
                              start=(k == 0), stop=(k == KD - 1))
                last.then_inc(done["e2"], 1)

            def len2(b):
                eng.wait_ge(done["cnt2"], b + 1)
                mm(bank("e2", b)[0:T, 400:401], cst[0:1, C_ONES:C_ONES + T], cnt[0:1, 1, b:b + 1],
                   start=True, stop=True).then_inc(done["len2"], 1)

            def p2T_(b):
                eng.wait_ge(done["exp2"], b + 1)
                ps = take_bank(eng, "p2T", b)
                for c in range(KS):
                    last = nc.tensor.transpose(ps[:, c * T:(c + 1) * T], p2[:, b % 4, c * P:(c + 1) * P],
                                               ident[0:T, 0:T])
                last.then_inc(done["p2T"], 1)

            def u_(j):
                eng.wait_ge(done["p2Tc"], 2 * j + 2)
                ps = take_bank(eng, "u", j)
                for i in range(2):
                    b = 2 * j + i
                    for c in range(KS):
                        last = mm(ps[0:T, i * D:(i + 1) * D], p2T[:, b % 4, c, :], context(j)[0][:, i, c, :],
                                  start=(c == 0), stop=(c == KS - 1))
                last.then_inc(done["u"], 1)

            def shared_up(name, which):
                def f(n):
                    j, q = n // 2, n % 2
                    eng.wait_ge(done["hTc"], j + 1)
                    eng.wait_ge(d_sh, 16)
                    ps = take_bank(eng, name, n)
                    for fi in range(2):
                        for k in range(KD):
                            w0 = which * KD * F + k * F + (2 * q + fi) * P
                            last = mm(ps[:, 2 * fi * T:2 * (fi + 1) * T], wshared[:, w0:w0 + P],
                                      featA[:, k, pair_cols(j)], start=(k == 0), stop=(k == KD - 1))
                    last.then_inc(done[name], 1)
                return f

            def sd(j):
                eng.wait_ge(done["hs"], 2 * j + 2)
                ps = take_bank(eng, "sd", j)
                for i in range(2):
                    for f in range(KF):
                        w0 = 2 * KD * F + f * D
                        last = mm(ps[0:T, i * D:(i + 1) * D], hs[:, f, toks(2 * j + i)], wshared[:, w0:w0 + D],
                                  start=(f == 0), stop=(f == KF - 1))
                last.then_inc(done["sd"], 1)

            def lg(_):
                eng.wait_ge(done["hTc"], PAIRS)
                eng.wait_ge(d_gate, 16)
                ps = take_bank(eng, "lg", 0)
                for b in range(B):
                    for k in range(KD):
                        last = mm(ps[0:T, b * E:(b + 1) * E], featA[:, k, toks(b)], gate_sb[:, k, :],
                                  start=(k == 0), stop=(k == KD - 1))
                last.then_inc(done["lg"], 1)

            def scT(_):
                eng.wait_ge(done["score"], 1)
                ps = take_bank(eng, "scT", 0)
                nc.tensor.transpose(ps[:, 0:T], score.rearrange("t b e -> t (b e)"),
                                    ident[0:T, 0:T]).then_inc(done["scT"], 1)

            def bc(j):
                eng.wait_ge(done["dix"], 1)
                eng.wait_ge(s_const, 1)
                ps = take_bank(eng, "bc", j)
                for i in range(2):
                    last = mm(ps[0:T, i * EC:(i + 1) * EC], bsel[:, 2 * j + i, :],
                              dix[:].rearrange("p e c -> p (e c)"), start=True, stop=True)
                last.then_inc(done["bc"], 1)

            def col(_):
                eng.wait_ge(done["dix"], 1)
                eng.wait_ge(s_const, 1)
                ps = take_bank(eng, "col", 0)
                for hf in range(2):
                    c = slice(hf * HALF * CAP, (hf + 1) * HALF * CAP)
                    mm(ps[0:HALF * CAP, 16 * hf:16 * hf + B], dix[:].rearrange("p e c -> p (e c)")[:, c], bcol[:],
                       start=True, stop=True)
                    last = mm(ps[0:HALF * CAP, 16 * hf + B:16 * hf + 2 * B], dw.rearrange("p e c -> p (e c)")[:, c],
                              cst[:, C_BATCH:C_BATCH + B], start=True, stop=True)
                last.then_inc(done["col"], 1)

            def gather(name, m):
                def f(j):
                    eng.wait_ge(done["sel"], j + 1)
                    eng.wait_ge(done["nm4"], j + 1)
                    ps = take_bank(eng, name, j)
                    for i in range(2):
                        b = 2 * j + i
                        last = mm(ps[:, i * EC:(i + 1) * EC], xn[:, b, m * P:(m + 1) * P], sel[:, b, :],
                                  start=True, stop=True)
                    last.then_inc(done[name], 1)
                return f

            def expert_up(name, which):
                def f(e):
                    if e == 0:
                        eng.wait_ge(done["xg0"], PAIRS)
                        eng.wait_ge(done["xg1"], PAIRS)
                    eng.wait_ge(d_we[e % RING], 16 * (e // RING + 1))
                    ps = take_bank(eng, name, e)
                    for f_ in range(KF):
                        for k in range(KD):
                            w0 = which * KD * F + k * F + f_ * P
                            last = mm(ps[:, f_ * SLOTS:(f_ + 1) * SLOTS], we[:, e % RING, w0:w0 + P],
                                      xg[:, k, e, :], start=(k == 0), stop=(k == KD - 1))
                    last.then_inc(done[name], 1)
                return f

            def down(e):
                eng.wait_ge(done["hE"], e + 1)
                ps = take_bank(eng, "D", e)
                for f in range(KF):
                    w0 = 2 * KD * F + f * D
                    last = mm(ps[0:SLOTS, 0:D], hE[:, e % 2, f * SLOTS:(f + 1) * SLOTS],
                              we[:, e % RING, w0:w0 + D], start=(f == 0), stop=(f == KF - 1))
                last.then_inc(done["D"], 1)

            def scat(n):
                hf, j = n // PAIRS, n % PAIRS
                for r in range(2):
                    eng.wait_ge(d_mv[r], 16 * (hf + 1) * (HALF // 2))
                eng.wait_ge(done["wsel"], 1)
                ps = take_bank(eng, "scat", n)
                for i in range(2):
                    b = 2 * j + i
                    last = mm(ps[0:T, i * D:(i + 1) * D], wsel[:, hf, b, :], eo_all[:, hf, b, :],
                              start=True, stop=True)
                last.then_inc(done["scat"], 1)

            do = dict(m1=fused_weights("m1", W_Q1T, W_K1T, d_w1), m2=fused_weights("m2", W_Q2T, W_K2T, d_w2),
                      xT=turn("xT", xn, "nm0"), gT=by_feature("gT", m1, featA, "xTc", (done["m1c"], 1)),
                      v=by_token("v", featA, wsm[:, W_V1], "xTc"), e1=e1, len1=len1, p1T=p1T_, z1=z1,
                      x1T=turn("x1T", rn[:, 1], "nm1"),
                      g2T=by_feature("g2T", m2, featA, "x1Tc", (done["m2c"], 1)), e2=e2, len2=len2, p2T=p2T_,
                      u=u_, uT=turn("uT", u, "uc"), z2=by_token("z2", uT, wsm[:, W_V2], "uTc"),
                      x2T=turn("x2T", rn[:, 1], "nm2"), f1=by_feature("f1", wsm[:, W_FC1], featA, "x2Tc"),
                      f2=by_token("f2", featB, wsm[:, W_FC2], "f1c"), hT=turn("hT", xn, "nm4"),
                      shG=shared_up("shG", 0), shU=shared_up("shU", 1), sd=sd, lg=lg, scT=scT, bc=bc, col=col,
                      ga0=gather("ga0", 0), ga1=gather("ga1", 1), G=expert_up("G", 0), U=expert_up("U", 1), D=down, scat=scat)
            for name, unit in ORDER:
                if name in do:
                    do[name](unit)

        @block.scalar
        def _(eng):
            act = nc.scalar.activation

            def fused_copy(name, dst):
                def f(_):
                    eng.wait_ge(done[name[:-1]], 1)
                    nc.scalar.copy(dst.rearrange("p k d -> p (k d)"), bank(name[:-1], 0)).then_inc(done[name], 1)
                return f

            def copy_pair(name, dst):
                def f(j):
                    eng.wait_ge(done[name], j + 1)
                    nc.scalar.copy(dst[:, :, pair_cols(j)],
                                   bank(name, j)[:, 0:4 * T].rearrange("p (k t) -> p k t", k=KD)
                                   ).then_inc(done[name + "c"], 1)
                return f

            def affine_pair(name, dst, func, bias, scale):
                def f(j):
                    eng.wait_ge(done[name], j + 1)
                    for k in range(KD):
                        last = act(dst[:, k, pair_cols(j)], bank(name, j)[:, 2 * k * T:2 * (k + 1) * T], func,
                                   bias=cst[:, bias + k:bias + k + 1],
                                   scale=cst[:, scale + k:scale + k + 1] if scale else 1.0)
                    last.then_inc(done[name + "c"], 1)
                return f

            def exp1(j):
                eng.wait_ge(done["mask1"], j + 1)
                for i in range(2):
                    b = 2 * j + i
                    last = act(p1[:, b, :], emk1[:, i, :], ACT.Exp, bias=nmax[:, 0, b:b + 1], scale=-1.0,
                               accum_out=rsum[:, 0, b:b + 1])
                last.then_inc(done["exp1"], 1)

            def p1Tc(j):
                eng.wait_ge(done["p1T"], j + 1)
                nc.scalar.copy(p1T[:, pair(j), :], bank("p1T", j)[0:T, 0:2 * T].rearrange("p (i t) -> p i t", i=2)
                               ).then_inc(done["p1Tc"], 1)

            def vc(j):
                eng.wait_ge(done["v"], j + 1)
                nc.scalar.copy(vbuf[:, pair(j), :], bank("v", j)[0:T, :].rearrange("p (i d) -> p i d", i=2)
                               ).then_inc(done["vc"], 1)

            def exp2(b):
                eng.wait_ge(done["mask2"], b + 1)
                if b == 0:
                    eng.wait_ge(s_const, 1)
                if b >= 4:
                    eng.wait_ge(done["p2T"], b - 3)
                act(p2[:, b % 4, 0:S], emk[:, b % 2, :], ACT.Exp, bias=nmax[:, 1, b:b + 1], scale=-1.0,
                    accum_out=rsum[:, 1, b:b + 1]).then_inc(done["exp2"], 1)

            def p2Tc(b):
                eng.wait_ge(done["p2T"], b + 1)
                if b >= 4:
                    eng.wait_ge(done["u"], (b - 4) // 2 + 1)
                nc.scalar.copy(p2T[:, b % 4], bank("p2T", b)[:, 0:KS * T].rearrange("p (c t) -> p c t", c=KS)
                               ).then_inc(done["p2Tc"], 1)

            def uc(j):
                eng.wait_ge(done["u"], j + 1)
                eng.wait_ge(done["inv2"], j + 1)
                for i in range(2):
                    b = 2 * j + i
                    last = act(u[:, b, :], bank("u", j)[0:T, i * D:(i + 1) * D], ACT.Copy,
                               scale=rinv[:, 1, b:b + 1])
                last.then_inc(done["uc"], 1)

            def lex_(_):
                eng.wait_ge(done["lsh"], 1)
                act(lex, lsh, ACT.Exp).then_inc(done["lex"], 1)

            def gel_(n):
                eng.wait_ge(done["shG"], n + 1)
                if n == 0:
                    eng.wait_ge(done["z1"], PAIRS)
                if n >= 2:
                    eng.wait_ge(done["hs"], n - 1)
                act(gel[:, n % 2, 0:4 * T], bank("shG", n)[:, 0:4 * T], ACT.Gelu).then_inc(done["gel"], 1)

            def xg1(j):
                eng.wait_ge(done["ga1"], j + 1)
                if j == 0:
                    eng.wait_ge(done["u"], 2)
                nc.scalar.copy(xg[:, 1].rearrange("p e (c b) -> p e c b", b=B)[:, :, :, pair(j)],
                   bank("ga1", j)[:, 0:2 * EC].rearrange("p (i e c) -> p e c i", i=2, e=E)
                   ).then_inc(done["xg1"], 1)

            def gelE(e):
                eng.wait_ge(done["G"], e + 1)
                if e >= 2:
                    eng.wait_ge(done["hE"], e - 1)
                else:
                    eng.wait_ge(done["hs"], 2 * PAIRS)
                act(gel[:, e % 2, 0:KF * SLOTS], bank("G", e)[:, 0:KF * SLOTS], ACT.Gelu).then_inc(done["gelE"], 1)

            def eo_(e):
                eng.wait_ge(done["D"], e + 1)
                if e >= 2:
                    eng.wait_ge(d_mv[e % 2], 16 * (e // 2))
                nc.scalar.copy(eo[:, e % 2, :], bank("D", e)[0:SLOTS, 0:D]).then_inc(done["eo"], 1)

            do = dict(m1c=fused_copy("m1c", m1), m2c=fused_copy("m2c", m2), xTc=copy_pair("xT", featA),
                      gTc=copy_pair("gT", featB), vc=vc, exp1=exp1, p1Tc=p1Tc,
                      x1Tc=affine_pair("x1T", featA, ACT.Identity, V_B1, V_G1), g2Tc=copy_pair("g2T", featB),
                      exp2=exp2, p2Tc=p2Tc, uc=uc, uTc=copy_pair("uT", uT),
                      x2Tc=affine_pair("x2T", featA, ACT.Identity, V_B2, V_G2),
                      f1c=affine_pair("f1", featB, ACT.Relu, V_FC1, None), hTc=copy_pair("hT", featA),
                      lex=lex_, gel=gel_, xg1=xg1, gelE=gelE, eo=eo_)
            for name, unit in ORDER:
                if name in do:
                    do[name](unit)

        @block.vector
        def _(eng):
            v_ = nc.vector
            chain = [0]

            def then(ins):
                chain[0] += 1
                ins.then_inc(k_dve, 1)
                eng.wait_ge(k_dve, chain[0])

            def stats(n, j, src, name):
                for i in range(2):
                    last = v_.bn_stats(st6[:, n, 2 * j + i, :], src[:, 2 * j + i, :])
                then(last)
                for i in range(2):
                    last = v_.bn_aggr(mv[:, n, 2 * j + i, :], st6[:, n, 2 * j + i, :])
                last.then_inc(done[name], 1)

            def nm(n, dst, src):
                def f(j):
                    eng.wait_ge(done[f"rs{n}"], j + 1)
                    for b in (2 * j, 2 * j + 1):
                        last = v_.tensor_scalar(dst[:, b, :], src[:, b, :], mv[:, n, b, 0:1], rstd[:, n, b, :],
                                                ALU.subtract, ALU.mult)
                    last.then_inc(done[f"nm{n}"], 1)
                return f

            def st0(j):
                eng.wait_ge(d_x[j], 16)
                stats(0, j, xres, "st0")

            counted = [None]

            def count(a, b, energies, name, value, signal):
                if counted[0]:
                    eng.wait_ge(*counted[0])
                n = energies.shape[-1]
                ins = v_.tensor_scalar(nz[0:1, 0:n], energies, 0.0, None, ALU.not_equal, ALU.add,
                                       accum_out=cnt[0:1, a, b:b + 1])
                if signal:
                    ins.then_inc(done[name], 1)
                    counted[0] = (done[name], value)
                else:
                    then(ins)
                    counted[0] = None

            def cnt1(j):
                eng.wait_ge(done["e1"], j + 1)
                for i in range(2):
                    count(0, 2 * j + i, bank("e1", j)[0:1, i * T:(i + 1) * T], "cnt1", j + 1, i == 1)

            def cnt2(b):
                eng.wait_ge(done["e2"], b + 1)
                count(1, b, bank("e2", b)[0:1, 0:S], "cnt2", b + 1, True)

            def mask(a, b, energies, length, key, pn, em):
                v_.reciprocal(linv[:, a, b:b + 1], length)
                then(v_.tensor_scalar(pn, key, length, FAR, ALU.is_ge, ALU.mult))
                return v_.tensor_tensor_reduce(em, energies, pn, -INV_SQRT_DK, 3.0e38, ALU.add, ALU.min,
                                               nmax[:, a, b:b + 1])

            def mask1(j):
                eng.wait_ge(done["len1"], j + 1)
                if j >= 1:
                    eng.wait_ge(done["exp1"], j)
                ps = bank("e1", j)
                for i in range(2):
                    last = mask(0, 2 * j + i, ps[0:T, i * T:(i + 1) * T], ps[0:T, 400 + i:401 + i],
                                cst[0:T, C_CAUSAL:C_CAUSAL + T], pen1[:, i, :], emk1[:, i, :])
                last.then_inc(done["mask1"], 1)

            def mask2(b):
                eng.wait_ge(done["len2"], b + 1)
                if b >= 2:
                    eng.wait_ge(done["exp2"], b - 1)
                ps = bank("e2", b)
                mask(1, b, ps[0:T, 0:S], ps[0:T, 400:401], cst[0:T, C_KEY:C_KEY + S], pen[:, b % 2, :],
                     emk[:, b % 2, :]).then_inc(done["mask2"], 1)

            def inv(a, name, ready):
                def f(j):
                    eng.wait_ge(*ready(j))
                    c = pair(j)
                    then(v_.reciprocal(rinv[:, a, c], rsum[:, a, c]))
                    v_.scalar_tensor_tensor(rinv[:, a, c], linv[:, a, c], 0.0, rinv[:, a, c], ALU.mult,
                                            ALU.add).then_inc(done[name], 1)
                return f

            def sum1(j):
                eng.wait_ge(done["inv1"], j + 1)
                eng.wait_ge(done["z1"], j + 1)
                for i in range(2):
                    b = 2 * j + i
                    last = v_.scalar_tensor_tensor(rn[:, 0, b, :], bank("z1", j)[0:T, i * D:(i + 1) * D],
                                                   rinv[:, 0, b:b + 1], xn[:, b, :], ALU.mult, ALU.add)
                then(last)
                stats(1, j, rn[:, 0], "sum1")

            def plain_sum(name, n, product, res, ready):
                def f(j):
                    eng.wait_ge(done[product], j + 1)
                    eng.wait_ge(done[ready], j + 1)
                    then(v_.tensor_tensor(rn[:, 0, pair(j), :],
                                          bank(product, j)[0:T, :].rearrange("p (i d) -> p i d", i=2),
                                          res[:, pair(j), :], ALU.add))
                    stats(n, j, rn[:, 0], name)
                return f

            def st4(j):
                eng.wait_ge(done["x3"], j + 1)
                stats(4, j, xres, "st4")

            def hs_(n):
                j, q = n // 2, n % 2
                eng.wait_ge(done["gel"], n + 1)
                eng.wait_ge(done["shU"], n + 1)
                if n == 0:
                    eng.wait_ge(done["u"], 2)
                v_.tensor_tensor(hs[:, 2 * q:2 * q + 2, pair_cols(j)],
                                 gel[:, n % 2, 0:4 * T].rearrange("p (f t) -> p f t", f=2),
                                 bank("shU", n)[:, 0:4 * T].rearrange("p (f t) -> p f t", f=2),
                                 ALU.mult).then_inc(done["hs"], 1)

            def add_to_result(ps, j, name):
                v_.tensor_tensor(xres[:, pair(j), :], ps[0:T, :].rearrange("p (i d) -> p i d", i=2),
                                 xres[:, pair(j), :], ALU.add).then_inc(done[name], 1)

            def y(j):
                eng.wait_ge(done["sd"], j + 1)
                add_to_result(bank("sd", j), j, "y")

            def fin(n):
                hf, j = n // PAIRS, n % PAIRS
                eng.wait_ge(done["scat"], n + 1)
                if hf == 0:
                    eng.wait_ge(done["y"], j + 1)
                else:
                    eng.wait_ge(done["fin"], j + 1)
                add_to_result(bank("scat", n), j, "fin")

            def lsh_(_):
                eng.wait_ge(done["lg"], 1)
                lg = bank("lg", 0)[0:T, 0:B * E].rearrange("p (b e) -> p b e", b=B)
                then(v_.tensor_reduce(lmx[:], lg, AX.X, ALU.max))
                v_.tensor_tensor(lsh, lg, lmx[:].unsqueeze(2).to_broadcast([T, B, E]),
                                 ALU.subtract).then_inc(done["lsh"], 1)

            def score_(_):
                eng.wait_ge(done["lex"], 1)
                then(v_.tensor_reduce(lsum[:], lex, AX.X, ALU.add))
                then(v_.reciprocal(lri[:], lsum[:]))
                v_.tensor_tensor(score, lex, lri[:].unsqueeze(2).to_broadcast([T, B, E]),
                                 ALU.mult).then_inc(done["score"], 1)

            def sc(_):
                eng.wait_ge(done["scT"], 1)
                v_.tensor_copy(sS[:], bank("scT", 0)[:, 0:T]).then_inc(done["sc"], 1)

            def dix_(_):
                eng.wait_ge(done["sc"], 1)
                then(v_.max(top[:, 0:8], sS[:]))
                v_.max_index(tix[:, 0:8], top[:, 0:8], sS[:])
                then(v_.match_replace(sS2[:], top[:, 0:8], sS[:], -1.0))
                then(v_.max(top[:, 8:16], sS2[:]))
                then(v_.max_index(tix[:, 8:16], top[:, 8:16], sS2[:]))
                then(v_.tensor_copy(tixf[:], tix[:]))
                em = cst[:, C_EMASK:C_EMASK + E].unsqueeze(2).to_broadcast([P, E, CAP])
                v_.tensor_tensor(dw, em, top[:, 0:CAP].unsqueeze(1).to_broadcast([P, E, CAP]), ALU.mult)
                v_.tensor_tensor(dix[:], em, tixf[:, 0:CAP].unsqueeze(1).to_broadcast([P, E, CAP]),
                                 ALU.mult).then_inc(done["dix"], 1)

            def sel_(j):
                eng.wait_ge(done["bc"], j + 1)
                v_.tensor_scalar(sel[:, pair(j), :],
                                 bank("bc", j)[0:T, 0:2 * EC].rearrange("p (i c) -> p i c", i=2),
                                 cst[0:T, C_ROW:C_ROW + 1], None, ALU.is_equal).then_inc(done["sel"], 1)

            def wcol_(_):
                eng.wait_ge(done["col"], 1)
                v_.tensor_copy(wcol[:].rearrange("p h a b -> p (h a b)"),
                               bank("col", 0)[0:HALF * CAP, 0:32]).then_inc(done["wcol"], 1)

            def wsel_(_):
                eng.wait_ge(done["wcol"], 1)
                for hf in range(2):
                    for b in range(B):
                        last = v_.tensor_scalar(wsel[:, hf, b, :], cst[0:HALF * CAP, C_KEY:C_KEY + T],
                                                wcol[:, hf, 0, b:b + 1], wcol[:, hf, 1, b:b + 1],
                                                ALU.is_equal, ALU.mult)
                last.then_inc(done["wsel"], 1)

            def xg0(j):
                eng.wait_ge(done["ga0"], j + 1)
                if j == 0:
                    eng.wait_ge(done["u"], 2)
                v_.tensor_copy(xg[:, 0].rearrange("p e (c b) -> p e c b", b=B)[:, :, :, pair(j)],
                   bank("ga0", j)[:, 0:2 * EC].rearrange("p (i e c) -> p e c i", i=2, e=E)
                   ).then_inc(done["xg0"], 1)

            def hE_(e):
                eng.wait_ge(done["gelE"], e + 1)
                eng.wait_ge(done["U"], e + 1)
                if e >= 2:
                    eng.wait_ge(done["D"], e - 1)
                v_.tensor_tensor(hE[:, e % 2, :], gel[:, e % 2, 0:KF * SLOTS], bank("U", e)[:, 0:KF * SLOTS],
                                 ALU.mult).then_inc(done["hE"], 1)

            do = dict(st0=st0, nm0=nm(0, xn, xres), cnt1=cnt1, mask1=mask1,
                      inv1=inv(0, "inv1", lambda j: (done["exp1"], j + 1)), sum1=sum1,
                      nm1=nm(1, rn[:, 1], rn[:, 0]), cnt2=cnt2, mask2=mask2,
                      inv2=inv(1, "inv2", lambda j: (done["exp2"], 2 * j + 2)),
                      sum2=plain_sum("sum2", 2, "z2", x1, "x1a"), nm2=nm(2, rn[:, 1], rn[:, 0]),
                      sum3=plain_sum("sum3", 3, "f2", vbuf, "x2a"), nm3=nm(3, rn[:, 1], rn[:, 0]), st4=st4,
                      nm4=nm(4, xn, xres), hs=hs_, y=y, fin=fin, lsh=lsh_, score=score_, sc=sc, dix=dix_,
                      sel=sel_, wcol=wcol_, wsel=wsel_, xg0=xg0, hE=hE_)
            prepared = False
            for name, unit in ORDER:
                if name == "cnt1" and not prepared:
                    v_.memset(p2[:, :, S:SP_], 0.0)
                    eng.wait_ge(d_cst, 16)
                    v_.tensor_copy(bcol[:], cst[:, C_BATCH:C_BATCH + B])
                    v_.tensor_copy(bsel[:], cst[:, C_BATCH:C_BATCH + B].unsqueeze(2).to_broadcast([P, B, T])
                                   ).then_inc(s_const, 1)
                    prepared = True
                if name in do:
                    do[name](unit)

        @block.gpsimd
        def _(eng):
            g_ = nc.gpsimd
            chain = [0]

            def then(ins):
                chain[0] += 1
                ins.then_inc(k_pool, 1)
                eng.wait_ge(k_pool, chain[0])

            def rs(n, ready):
                def f(j):
                    eng.wait_ge(done[ready], j + 1)
                    then(g_.tensor_scalar_add(ve[:, n, pair(j), :], mv[:, n, pair(j), 1:2], EPS))
                    g_.tensor_tensor(rstd[:, n, pair(j), :], ve[:, n, pair(j), :], nhalf[:],
                                     ALU.pow).then_inc(done[f"rs{n}"], 1)
                return f

            def affine(name, ready, dst, g, b):
                def f(j):
                    eng.wait_ge(done[ready], j + 1)
                    if name == "x1a" and j == 0:
                        eng.wait_ge(d_row, 16)
                    then(g_.tensor_tensor(dst[:, pair(j), :], rn[:, 1, pair(j), :], bcast_row(g), ALU.mult))
                    g_.tensor_tensor(dst[:, pair(j), :], dst[:, pair(j), :], bcast_row(b),
                                     ALU.add).then_inc(done[name], 1)
                return f

            fc2_bias = [False]

            def x2a(j):
                if not fc2_bias[0]:
                    fc2_bias[0] = True
                    then(g_.tensor_tensor(row[:, R_B2, :], row[:, R_B2, :], row[:, R_FC2, :], ALU.add))
                affine("x2a", "nm2", vbuf, R_G2, R_B2)(j)

            def xb(j):
                eng.wait_ge(done["nm0"], j + 1)
                if j == 0:
                    eng.wait_ge(d_row, 16)
                g_.tensor_tensor(xres[:, pair(j), :], xres[:, pair(j), :], bcast_row(R_B3),
                                 ALU.add).then_inc(done["xb"], 1)

            def x3(j):
                eng.wait_ge(done["nm3"], j + 1)
                eng.wait_ge(done["xb"], j + 1)
                then(g_.tensor_tensor(rn[:, 1, pair(j), :], rn[:, 1, pair(j), :], bcast_row(R_G3), ALU.mult))
                g_.tensor_tensor(xres[:, pair(j), :], xres[:, pair(j), :], rn[:, 1, pair(j), :],
                                 ALU.add).then_inc(done["x3"], 1)

            then(g_.memset(nhalf[:], -0.5))
            do = dict(rs0=rs(0, "st0"), rs1=rs(1, "sum1"), x1a=affine("x1a", "nm1", x1, R_G1, R_B1),
                      rs2=rs(2, "sum2"), x2a=x2a, rs3=rs(3, "sum3"), xb=xb, x3=x3, rs4=rs(4, "st4"))
            for name, unit in ORDER:
                if name in do:
                    do[name](unit)


_NAMES = ("x", "ctx_tok", "ctx_feat", "w_small", "consts", "rows", "gate", "w_moe")


def kernel(**inputs):
    import numpy as _np
    import concourse.bacc as _bacc
    from concourse import mybir as _mybir
    from concourse.bass_utils import run_bass_kernel_spmd as _run

    a = {k: _np.asarray(v) for k, v in inputs.items()}
    f32 = _np.float32

    def chunked(w):
        return w.reshape(-1, P, w.shape[1]).transpose(1, 0, 2)

    def vec(v):
        return v.reshape(KD, P).T

    ctx = a["ctx_1024"]
    ctx_tok = _np.concatenate([ctx, _np.zeros((B, SP_ - S, D), f32)], axis=1)
    ctx_tok = ctx_tok.reshape(B, KS, P, D).transpose(2, 0, 1, 3)
    ctx_feat = ctx.reshape(B, S, KD, P).transpose(3, 0, 2, 1)
    w_small = _np.stack([chunked(w) for w in (
        a["L0_xattn_Wq1"].T, a["L0_xattn_Wk1"].T, a["L0_xattn_Wv1"], a["L0_xattn_Wq2"].T, a["L0_xattn_Wk2"].T,
        a["L0_xattn_Wv2"], a["L0_xattn_fc1_w"], a["L0_xattn_fc2_w"])], axis=1)
    part = _np.arange(P)
    key = _np.arange(S)
    causal = _np.where(key[None, :T] > part[:, None], 4 * S, key[None, :T])
    consts = _np.concatenate([
        _np.eye(P), causal, _np.broadcast_to(key, (P, S)), part[:, None],
        part[:, None] % E == _np.arange(E)[None], part[:, None] // E == _np.arange(B)[None],
        _np.ones((P, T))], axis=1).astype(f32)
    consts = _np.concatenate([consts] + [vec(a["L0_xattn_" + n]) for n in
                                         ("ln1_g", "ln1_b", "ln2_g", "ln2_b", "fc1_b")], axis=1)
    rows = _np.stack([a["L0_xattn_" + n] for n in ("ln1_g", "ln1_b", "ln2_g", "ln2_b", "ln3_g", "ln3_b", "fc2_b")])
    gate = chunked(a["L0_ffn_gate_w"].T)

    def moe(g, u, d):
        return _np.concatenate([chunked(w.T).reshape(P, -1) for w in (g, u, d)], axis=1)

    w_moe = _np.stack([moe(a["L0_ffn_Wg"][e], a["L0_ffn_Wu"][e], a["L0_ffn_Wd"][e]) for e in range(E)]
                      + [moe(a["L0_ffn_Ws_g"], a["L0_ffn_Ws_u"], a["L0_ffn_Ws_d"])])
    data = dict(x=a["x"], ctx_tok=ctx_tok, ctx_feat=ctx_feat, w_small=w_small, consts=consts, rows=rows,
                gate=gate, w_moe=w_moe)

    nc = _bacc.Bacc("TRN2", target_bir_lowering=False, num_devices=1)
    arrays, args = {}, []
    for name in _NAMES:
        arr = _np.ascontiguousarray(data[name])
        arrays[f"in_{name}"] = arr
        args.append(nc.dram_tensor(f"in_{name}", arr.shape, _mybir.dt.from_np(arr.dtype), kind="ExternalInput").ap())
    args.append(nc.dram_tensor("out_0", (B, T, D), F32, kind="ExternalOutput").ap())
    xattn_moe(nc, *args)
    r = _run(nc, [arrays], core_ids=[0])
    return r.results[0]["out_0"]
```

```python
from contextlib import ExitStack

import concourse.bass as bass
from concourse import mybir

ALU = mybir.AluOpType
ACT = mybir.ActivationFunctionType
AX = mybir.AxisListType
F32 = mybir.dt.float32
F32R = mybir.dt.float32r
BF16 = mybir.dt.bfloat16
U32 = mybir.dt.uint32

P = 128
B, T, D = 8, 100, 256
S = 361
NT = B * T
KD = D // P
KS = -(-S // P)
SP_ = KS * P
PAIRS = B // 2
E, F = 16, 512
KF = F // P
CAP = int(T * 2.0 / E)
SLOTS = B * CAP
HALF = E // 2
EC = E * CAP
INV_SQRT_DK = 1.0 / (D // 16) ** 0.5
EPS = 1e-5
FAR = -3.0e38
WE = 2 * KD * F + KF * D
RING = 4
BANKS = 8

C_IDENT = 0
C_CAUSAL = C_IDENT + P
C_KEY = C_CAUSAL + T
C_ROW = C_KEY + S
C_EMASK = C_ROW + 1
C_BATCH = C_EMASK + E
C_ONES = C_BATCH + B
C_VEC = C_ONES + T
C_END = C_VEC + 5 * KD
V_G1, V_B1, V_G2, V_B2, V_FC1 = (C_VEC + KD * i for i in range(5))
R_G1, R_B1, R_G2, R_B2, R_G3, R_B3, R_FC2 = range(7)
W_Q1T, W_K1T, W_V1, W_Q2T, W_K2T, W_V2, W_FC1, W_FC2 = range(8)

TENSOR_ORDER = """
m1.0@0 xT.0@1 xT.1@2 gT.0@3 gT.1@4 e1.0@5 v.0@6 len1.0 e1.1@7 xT.2@0 v.1@1 p1T.0@2 xT.3@3 len1.1 m2.0@4 z1.0@6
gT.2@5 p1T.1@1 gT.3@2 z1.1@0 e1.2@3 x1T.0@7 v.2@4 g2T.0@5 len1.2 e1.3@6 x1T.1@1 e2.0@2 e2.1@0 p1T.2@7 len1.3 len2.0
g2T.1@4 z1.2@5 len2.1 v.3@3 p2T.0@1 p1T.3@7 e2.2@6 z1.3@4 x1T.2@2 p2T.1@5 e2.3@3 len2.2 g2T.2@1 u.0@7 p2T.2@0
x1T.3@2 len2.3 e2.4@5 e2.5@4 uT.0@6 p2T.3@1 len2.4 g2T.3@0 z2.0@2 p2T.4@3 u.1@7 len2.5 e2.6@1 uT.1@6 e2.7@5 z2.1@0
p2T.5@3 x2T.0@2 len2.6 len2.7 u.2@7 f1.0@4 p2T.6@6 x2T.1@3 uT.2@2 p2T.7@0 f2.0@1 z2.2@5 u.3@7 f1.1@4 x2T.2@6 uT.3@2
f2.1@0 z2.3@3 f1.2@1 f2.2@5 x2T.3@7 hT.0@4 f1.3@2 f2.3@6 hT.1@0 shG.0@3 shG.1@1 shG.2@7 shG.3@4 hT.2@5 shU.0@2
shU.1@0 shU.2@6 hT.3@3 shU.3@1 lg.0@7 shG.4@4 shG.5@5 shU.4@2 shG.6@0 shG.7@6 scT.0@3 shU.5@1 shU.6@7 shU.7@4
slot.0@5 bc.0@2 bc.1@0 bc.2@3 bc.3@6 sd.0@5 ga0.0@1 ga0.1@7 ga0.2@4 ga0.3@2 ga1.0@0 ga1.1@3 ga1.2@6 ga1.3@1 col.0@7
sd.1@4 U.0@2 G.0@0 sd.2@3 hET.0@6 sd.3@7 U.1@1 G.1@0 D.0@2 U.2@6 hET.1@5 G.2@4 G.3@3 U.3@7 hET.2@0 D.1@1 U.4@2
hET.3@5 D.2@4 G.4@6 G.5@3 U.5@7 hET.4@1 D.3@0 hET.5@5 U.6@4 G.6@6 D.4@2 U.7@3 hET.6@7 G.7@0 D.5@1 U.8@5 hET.7@6
D.6@4 G.8@2 U.9@7 D.7@0 hET.8@1 G.9@3 U.10@6 D.8@4 hET.9@2 G.10@5 G.11@0 D.9@1 hET.10@3 U.11@7 G.12@4 D.10@2
hET.11@5 U.12@6 G.13@0 hET.12@1 D.11@3 U.13@7 G.14@4 hET.13@2 U.14@6 D.12@5 D.13@0 hET.14@3 G.15@7 U.15@1 D.14@4
hET.15@2 D.15@6 scat.0@5 scat.1@0 scat.2@3 scat.3@7 scat.4@1 scat.5@4 scat.6@2 scat.7@6
"""
SCALAR_ORDER = """
m1c.0 xTc.0 xTc.1 gTc.0 gTc.1 vc.0 exp1.0 vc.1 p1Tc.0 xTc.2 xTc.3 exp1.1 m2c.0 gTc.2 p1Tc.1 gTc.3 x1Tc.0 vc.2 g2Tc.0
x1Tc.1 exp1.2 p1Tc.2 g2Tc.1 exp1.3 exp2.0 vc.3 p2Tc.0 p1Tc.3 exp2.1 x1Tc.2 p2Tc.1 g2Tc.2 exp2.2 p2Tc.2 x1Tc.3 uc.0
exp2.3 p2Tc.3 uTc.0 g2Tc.3 exp2.4 p2Tc.4 uc.1 uTc.1 exp2.5 p2Tc.5 x2Tc.0 exp2.6 uc.2 exp2.7 f1c.0 p2Tc.6 uTc.2
p2Tc.7 x2Tc.1 uc.3 f1c.1 uTc.3 shi.0 shi.1 shi.2 x2Tc.2 f1c.2 shi.3 shi.4 shi.5 x2Tc.3 hTc.0 hhi.0 f1c.3 hTc.1 hhi.1
gel.0 gel.1 gel.2 gel.3 hTc.2 hhi.2 hsh.0 whG.0 hTc.3 hhi.3 whU.0 hsh.1 hsh.2 hsh.3 whU.1 lex.0 gel.4 gel.5 gel.6
gel.7 hsh.4 whG.1 whD.0 whD.1 hsh.5 hsh.6 hsh.7 xgh0.0 xgh0.1 xgh0.2 xgh0.3 xgh1.0 xgh1.1 xgh1.2 xgh1.3 whU.2 gelE.0
whG.2 hEh.0 whU.3 gelE.1 whG.3 eo.0 whD.2 hEh.1 gelE.2 whU.4 gelE.3 whG.4 hEh.2 whG.5 eo.1 whD.3 hEh.3 whU.5 eo.2
whD.4 gelE.4 whU.6 gelE.5 whG.6 hEh.4 whU.7 hEh.5 eo.3 whG.7 whD.5 gelE.6 whU.8 eo.4 whD.6 hEh.6 whG.8 gelE.7 whU.9
eo.5 whD.7 hEh.7 whG.9 eo.6 whD.8 gelE.8 whU.10 whG.10 eo.7 hEh.8 whD.9 gelE.9 whG.11 whU.11 eo.8 hEh.9 whD.10
gelE.10 whG.12 gelE.11 whU.12 eo.9 hEh.10 whD.11 whG.13 gelE.12 whU.13 hEh.11 eo.10 whD.12 whG.14 gelE.13 whU.14
whD.13 hEh.12 eo.11 whG.15 gelE.14 hEh.13 whU.15 whD.14 eo.12 eo.13 hEh.14 whD.15 gelE.15 eo.14 hEh.15 eo.15
"""
VECTOR_ORDER = """
st0.0 st0.1 nm0.0 nm0.1 st0.2 nm0.2 const.0 st0.3 cnt1.0 mask1.0 nm0.3 cnt1.1 mask1.1 inv1.0 inv1.1 sum1.0 nm1.0
sum1.1 cnt1.2 nm1.1 mask1.2 cnt2.0 cnt1.3 cnt2.1 mask1.3 mask2.0 inv1.2 sum1.2 inv1.3 mask2.1 nm1.2 cnt2.2 sum1.3
cnt2.3 mask2.2 inv2.0 nm1.3 mask2.3 cnt2.4 cnt2.5 inv2.1 mask2.4 sum2.0 nm2.0 mask2.5 cnt2.6 cnt2.7 inv2.2 sum2.1
mask2.6 mask2.7 nm2.1 inv2.3 sum3.0 sum2.2 nm3.0 nm2.2 x3.0 st4.0 slo.0 slo.1 sum3.1 sum2.3 nm3.1 nm4.0 nm2.3 slo.2
x3.1 st4.1 sum3.2 hlo.0 nm4.1 nm3.2 slo.3 sum3.3 hlo.1 x3.2 st4.2 nm3.3 slo.4 nm4.2 slo.5 x3.3 st4.3 hs.0 hlo.2
nm4.3 hs.1 hs.2 wlG.0 hs.3 hlo.3 wlU.0 lsh.0 hsl.0 hsl.1 hsl.2 hsl.3 score.0 hs.4 sc.0 dix.0 top3.0 hsl.4 score3.0
hs.5 hs.6 hs.7 sel.0 sel.1 sel.2 sel.3 hsl.5 hsl.6 xgl0.0 xgl0.1 xgl0.2 xgl0.3 xgl1.0 xgl1.1 xgl1.2 wcol.0 hsl.7
xgl1.3 wlG.1 wlU.1 wsel.0 hE.0 wlG.2 wlU.2 hEl.0 y.0 y.1 y.2 y.3 hE.1 wlU.3 wlG.3 hEl.1 hE.2 wlU.4 hE.3 wlG.4 hEl.2
wlG.5 hEl.3 wlU.5 hE.4 wlU.6 hE.5 wlG.6 wlU.7 hEl.4 hEl.5 wlG.7 hE.6 wlU.8 hEl.6 wlG.8 hE.7 wlU.9 hEl.7 wlG.9 hE.8
wlU.10 wlG.10 hEl.8 hE.9 wlG.11 wlU.11 hEl.9 hE.10 wlG.12 wlU.12 hEl.10 hE.11 wlG.13 wlU.13 hE.12 hEl.11 wlG.14
wlU.14 hE.13 hEl.12 wlG.15 hEl.13 hE.14 wlU.15 hEl.14 hE.15 hEl.15 fin.0 fin.1 fin.2 fin.3 fin.4 fin.5 fin.6 fin.7
"""
POOL_ORDER = """
rs0.0 rs0.1 rs0.2 rs0.3 xb.0 xb.1 xb.2 xb.3 rs1.0 x1a.0 rs1.1 x1a.1 rs1.2 x1a.2 rs1.3 x1a.3 rs2.0 x2a.0 rs2.1 x2a.1
rs3.0 rs2.2 x3m.0 x2a.2 rs4.0 rs3.1 rs2.3 x3m.1 x2a.3 rs4.1 rs3.2 x3m.2 rs3.3 rs4.2 x3m.3 rs4.3 wlD.0 wlD.1 wlD.2
wlD.3 wlD.4 wlD.5 wlD.6 wlD.7 wlD.8 wlD.9 wlD.10 wlD.11 wlD.12 wlD.13 wlD.14 wlD.15
"""
LAST_READER = {
    "m1": "m1c", "m2": "m2c", "xT": "xTc", "gT": "gTc", "v": "vc", "e1": "mask1", "p1T": "p1Tc", "z1": "sum1",
    "x1T": "x1Tc", "g2T": "g2Tc", "e2": "mask2", "p2T": "p2Tc", "u": "uc", "uT": "uTc", "z2": "sum2", "x2T":
    "x2Tc", "f1": "f1c", "f2": "sum3", "hT": "hTc", "sd": "y", "bc": "sel", "shG": "gel", "shU": "hs", "lg":
    "lsh", "scT": "sc", "col": "wcol", "slot": "score3", "ga0": "xgl0", "ga1": "xgl1", "G": "gelE", "U": "hE",
    "hET": "hEl", "D": "eo", "scat": "fin"
}


def read_order(text):
    order, banks, holder = [], {}, {}
    for item in text.split():
        step, _, bank = item.partition("@")
        name, unit = step.split(".")
        order.append((name, int(unit)))
        if bank:
            banks[order[-1]] = (int(bank), holder.get(bank))
            holder[bank] = order[-1]
    return order, banks


def xattn_moe(nc, x, ctx_tok, ctx_feat, w_small, consts, rows, gate, w_moe, out):
    stack = ExitStack()
    with stack:
        def sb(name, shape, dt=F32):
            return stack.enter_context(nc.sbuf_tensor(name, shape, dt))

        def sem(name):
            return stack.enter_context(nc.semaphore(name))

        cst = sb("cst", [P, C_END])


        def slab(name, cols, *stays):
            made = []
            for tensors in stays:
                with ExitStack() as stay:
                    made.append([stay.enter_context(nc.sbuf_tensor(n, shape, dt)) for n, shape, dt in tensors])
            sb(name, [P, cols])
            return made

        (wsm,), (whi0,) = slab("slab_w", 8 * KD * D, [("wsm", [P, 8, KD, D], F32)], [("whi0", [P, WE], F32R)])
        (row, cross), (whi1,) = slab("slab_r", 7 * D + 4 * SP_,
                                     [("row", [P, 7, D], F32), ("cross", [P, 4, SP_], F32)],
                                     [("whi1", [P, WE], F32R)])
        whi = (whi0, whi1)
        (uT,), (hhi,), (hTh, hTl) = slab("slab_u", KD * NT, [("uT", [P, KD, NT], F32)],
                                         [("hhi", [P, KD, NT], F32R)],
                                         [("hTh", [P, 2, KF * SLOTS], F32R), ("hTl", [P, 2, KF * SLOTS], F32R)])
        (p2T, masks), (hlo, eo) = slab(
            "slab_p", 4 * KS * T + 4 * S, [("p2T", [P, 4, KS, T], F32), ("masks", [P, 2, 2, S], F32)],
            [("hlo", [P, KD, NT], F32R), ("eo", [SLOTS, 2, D], F32)])
        m1 = wsm[:, W_Q1T]
        m2 = wsm[:, W_Q2T]
        gate_sb = sb("gate_sb", [P, KD, E])
        xres = sb("xres", [T, B, D])
        xn = sb("xn", [T, B, D])
        featA = sb("featA", [P, KD, NT])
        (featB,), (hs0_lo,), (wsel,) = slab("slab_b", KD * NT, [("featB", [P, KD, NT], F32)],
                                           [("hs0_lo", [P, KF, 4 * T], F32R)],
                                           [("wsel", [HALF * CAP, 2, B, T], F32)])
        vbuf = sb("vbuf", [T, B, D])
        (rn_all,), (hs1_hi, hs1_lo) = slab("slab_n", 2 * B * D, [("rn_all", [P, 2, B, D], F32)],
                                           [(n, [P, KF, 4 * T], F32R) for n in ("hs1_hi", "hs1_lo")])
        eo_all = rn_all[0:HALF * CAP]
        rn = rn_all[0:T]
        (x1_all,), (hs0_hi,) = slab("slab_1", B * D, [("x1_all", [P, B, D], F32)],
                                    [("hs0_hi", [P, KF, 4 * T], F32R)])
        x1 = x1_all[0:T]
        pen = masks[0:T, 0]
        emk = masks[0:T, 1]
        probs = sb("probs", [P, 2, B, T])
        p1 = probs[0:T, 0]
        p1T = probs[0:T, 1]
        p2 = cross[0:T]
        pen1 = cross[0:T, 2, 0:2 * T].rearrange("p (i t) -> p i t", i=2)
        emk1 = cross[0:T, 3, 0:2 * T].rearrange("p (i t) -> p i t", i=2)
        u = rn[:, 0]
        (we,), (we_lo,) = slab("slab_e", RING * WE, [("we", [P, RING, WE], F32)], [("we_lo", [P, RING, WE], F32R)])
        (region,), (xgh, xgl) = slab("slab_x", 2 * WE, [("region", [P, 2 * WE], F32)],
                                     [("xgh", [P, KD, E, SLOTS], F32R), ("xgl", [P, KD, E, SLOTS], F32R)])

        def context(j):
            place = region[:, j * WE:(j + 1) * WE] if j < 2 else we[:, j, :]
            n = 2 * KS * D
            return (place[:, 0:n].rearrange("p (b c d) -> p b c d", b=2, c=KS),
                    place[:, n:n + 2 * KD * S].rearrange("p (b k s) -> p b k s", b=2, k=KD))

        (wshared,), (ws_lo,) = slab("slab_s", WE, [("wshared", [P, WE], F32)], [("ws_lo", [P, WE], F32R)])
        ws_hi = we_lo[:, RING - 1]
        st6 = sb("st6", [T, 5, B, 6])
        mv = sb("mv", [T, 5, B, 2])
        ve = sb("ve", [T, 5, B, 1])
        rstd = sb("rstd", [T, 5, B, 1])
        nhalf = sb("nhalf", [T, 2, 1])
        nz = sb("nz", [1, S])
        cnt = sb("cnt", [1, 2, B])
        nmax = sb("nmax", [T, 2, B])
        rsum = sb("rsum", [T, 2, B])
        rinv = sb("rinv", [T, 2, B])
        linv = sb("linv", [T, 2, B])
        sel = vbuf[:].rearrange("t b d -> t (b d)")[:, 0:B * EC].rearrange("t (b c) -> t b c", b=B)
        late = probs[:].rearrange("p a b t -> p (a b t)")
        hs_hi, hs_lo = (hs0_hi, hs1_hi), (hs0_lo, hs1_lo)
        gel_s = late[:, 0:4 * 4 * T].rearrange("p (r c) -> p r c", r=4)
        gel = late[:, 0:2 * F].rearrange("p (r c) -> p r c", r=2)
        hE = x1_all[:].rearrange("p b d -> p (b d)")[0:SLOTS, 0:2 * F].rearrange("p (r c) -> p r c", r=2)
        warm = sb("warm", [P, 512], BF16)
        lmx = sb("lmx", [T, B])
        gate_rows = vbuf[:].rearrange("t b d -> t (b d)")[:, B * EC:B * EC + 3 * B * E].rearrange(
            "t (a b e) -> t a b e", a=3, b=B)
        lsh = gate_rows[:, 0]
        lex = gate_rows[:, 1]
        score = gate_rows[:, 2]
        lsum = sb("lsum", [T, B])
        lri = sb("lri", [T, B])
        sS = sb("sS", [P, T])
        sS2 = sb("sS2", [P, T])
        top = sb("top", [P, 16])
        tix = sb("tix", [P, 16], U32)
        tixf = sb("tixf", [P, 16])
        dix = sb("dix", [P, E, CAP], BF16)
        top3 = sb("top3", [P, CAP, B])
        score3 = sb("score3", [SLOTS, E])
        bsel = sb("bsel", [P, B, T], BF16)
        bcol = sb("bcol", [P, B], BF16)
        wcol = sb("wcol", [HALF * CAP, 2, B])

        psum = stack.enter_context(nc.psum_tensor("psum", [P, BANKS, 512], F32))

        ident = cst[:, C_IDENT:C_IDENT + P]

        d_x = [sem(f"d_x{j}") for j in range(PAIRS)]
        d_cst, d_w1, d_v1, d_w2, d_row, d_gate, d_sh, d_out = (
            sem(n) for n in ("d_cst", "d_w1", "d_v1", "d_w2", "d_row", "d_gate", "d_sh", "d_out"))
        d_ck = [sem(f"d_ck{j}") for j in range(PAIRS)]
        d_up = [sem(f"d_up{i}") for i in range(RING)]
        d_down = [sem(f"d_down{i}") for i in range(RING)]
        d_mv = [sem(f"d_mv{i}") for i in range(2)]
        s_warm = sem("s_warm")
        k_dve, k_pool = sem("k_dve"), sem("k_pool")

        tensor_order, banks = read_order(TENSOR_ORDER)
        scalar_order, vector_order, pool_order = (read_order(t)[0] for t in (SCALAR_ORDER, VECTOR_ORDER, POOL_ORDER))
        done = {name: sem("done_" + name) for name in dict.fromkeys(
            name for name, _ in tensor_order + scalar_order + vector_order + pool_order)}

        def bank(name, unit):
            return psum[:, banks[(name, unit)][0], :]

        def take_bank(eng, name, unit):
            before = banks[(name, unit)][1]
            if before is not None:
                eng.wait_ge(done[LAST_READER[before[0]]], before[1] + 1)
            return bank(name, unit)

        def toks(b):
            return slice(b * T, (b + 1) * T)

        def pair_cols(j):
            return slice(2 * j * T, (2 * j + 2) * T)

        def pair(j):
            return slice(2 * j, 2 * j + 2)

        def part_cols(part):
            n = {"G": 0, "U": 1, "D": 2}[part] * KD * F
            return slice(n, n + KD * F)

        def bcast_row(r):
            return row[0:T, r, :].unsqueeze(1).to_broadcast([T, 2, D])

        block = stack.enter_context(nc.Block())

        @block.sync
        def _(sp):
            xv = x.rearrange("b t d -> t b d")

            def load_ctx(j):
                ctxk, ctxf = context(j)
                sp.dma_start(ctxf, ctx_feat[:, pair(j)]).then_inc(d_ck[j], 16)
                sp.dma_start(ctxk, ctx_tok[:, pair(j)]).then_inc(d_ck[j], 16)

            def load_up(e):
                if e >= RING:
                    sp.wait_ge(done["G"], e - RING + 1)
                    sp.wait_ge(done["U"], e - RING + 1)
                elif e == RING - 1:
                    sp.wait_ge(done["shG"], 2 * KF)
                    sp.wait_ge(done["shU"], 2 * KF)
                elif e >= 2:
                    sp.wait_ge(done["u"], e + 1)
                    sp.wait_ge(done["e2"], 2 * e + 2)
                cols = slice(0, 2 * KD * F)
                sp.dma_start(we[:, e % RING, cols], w_moe[e, :, cols]).then_inc(d_up[e % RING], 16)

            def load_down(e):
                if e >= RING:
                    sp.wait_ge(done["D"], e - RING + 1)
                elif e == RING - 1:
                    sp.wait_ge(done["sd"], PAIRS)
                cols = part_cols("D")
                sp.dma_start(we[:, e % RING, cols], w_moe[e, :, cols]).then_inc(d_down[e % RING], 16)

            sp.dma_start(wsm[:, 0:2], w_small[:, 0:2]).then_inc(d_w1, 16)
            for j in range(PAIRS):
                sp.dma_start(xres[:, pair(j), :], xv[:, pair(j), :]).then_inc(d_x[j], 16)
                if j == 1:
                    sp.dma_start(cst[:], consts).then_inc(d_cst, 16)
            sp.dma_start(wsm[:, W_V1], w_small[:, W_V1]).then_inc(d_v1, 16)
            sp.dma_start(wsm[:, W_V1 + 1:], w_small[:, W_V1 + 1:]).then_inc(d_w2, 16)
            sp.dma_start(row[:], rows.partition_broadcast(P)).then_inc(d_row, 16)
            for j in range(PAIRS):
                load_ctx(j)
            sp.dma_start(gate_sb[:], gate).then_inc(d_gate, 16)
            sp.dma_start(wshared[:], w_moe[E]).then_inc(d_sh, 16)
            for e in range(RING):
                load_up(e)
                load_down(e)
            load_up(RING)

            for e in range(E):
                if e + RING + 1 < E:
                    load_up(e + RING + 1)
                sp.wait_ge(done["eo"], e + 1)
                if e == 0:
                    sp.wait_ge(done["sd"], PAIRS)
                r0 = (e % HALF) * CAP
                sp.dma_start(eo_all[r0:r0 + CAP, e // HALF], eo[:, e % 2, :]).then_inc(d_mv[e % 2], 16)
                if e + RING < E:
                    load_down(e + RING)

            ov = out.rearrange("b t d -> t b d")
            for j in range(PAIRS):
                sp.wait_ge(done["fin"], PAIRS + j + 1)
                sp.dma_start(ov[:, pair(j), :], xres[:, pair(j), :]).then_inc(d_out, 16)
            sp.wait_ge(d_out, 16 * PAIRS)

        @block.tensor
        def _(eng):
            mm = nc.tensor.matmul

            def fused_weights(name, wq, wk, loaded):
                def f(_):
                    eng.wait_ge(loaded, 16)
                    ps = take_bank(eng, name, 0)
                    for m in range(KD):
                        for k in range(KD):
                            last = mm(ps[:, m * D:(m + 1) * D], wsm[:, wq, k, m * P:(m + 1) * P], wsm[:, wk, k, :],
                                      start=(k == 0), stop=(k == KD - 1))
                    last.then_inc(done[name], 1)
                return f

            def turn(name, src, ready):
                def f(j):
                    eng.wait_ge(done[ready], j + 1)
                    if name == "xT" and j == 0:
                        eng.wait_ge(d_cst, 16)
                    ps = take_bank(eng, name, j)
                    for k in range(KD):
                        for i in range(2):
                            c0 = (2 * k + i) * T
                            last = nc.tensor.transpose(ps[:, c0:c0 + T], src[:, 2 * j + i, k * P:(k + 1) * P],
                                                       ident[0:T, 0:T])
                    last.then_inc(done[name], 1)
                return f

            def by_feature(name, w, rhs, ready, weights=None):
                def f(j):
                    if weights and j == 0:
                        eng.wait_ge(*weights)
                    eng.wait_ge(done[ready], j + 1)
                    ps = take_bank(eng, name, j)
                    for m in range(KD):
                        for k in range(KD):
                            last = mm(ps[:, 2 * m * T:2 * (m + 1) * T], w[:, k, m * P:(m + 1) * P],
                                      rhs[:, k, pair_cols(j)], start=(k == 0), stop=(k == KD - 1))
                    last.then_inc(done[name], 1)
                return f

            def by_token(name, lhs, w, ready):
                def f(j):
                    if j == 0:
                        eng.wait_ge(d_v1 if name == "v" else d_w2, 16)
                    eng.wait_ge(done[ready], j + 1)
                    ps = take_bank(eng, name, j)
                    for i in range(2):
                        for k in range(KD):
                            last = mm(ps[0:T, i * D:(i + 1) * D], lhs[:, k, toks(2 * j + i)], w[:, k, :],
                                      start=(k == 0), stop=(k == KD - 1))
                    last.then_inc(done[name], 1)
                return f

            def e1(j):
                eng.wait_ge(done["gTc"], j + 1)
                ps = take_bank(eng, "e1", j)
                for i in range(2):
                    b = 2 * j + i
                    for k in range(KD):
                        last = mm(ps[0:T, i * T:(i + 1) * T], featB[:, k, toks(b)], featA[:, k, toks(b)],
                                  start=(k == 0), stop=(k == KD - 1))
                last.then_inc(done["e1"], 1)

            def len1(j):
                eng.wait_ge(done["cnt1"], j + 1)
                mm(bank("e1", j)[0:T, 400:402], cst[0:1, C_ONES:C_ONES + T], cnt[0:1, 0, pair(j)],
                   start=True, stop=True).then_inc(done["len1"], 1)

            def p1T_(j):
                eng.wait_ge(done["exp1"], j + 1)
                ps = take_bank(eng, "p1T", j)
                for i in range(2):
                    last = nc.tensor.transpose(ps[0:T, i * T:(i + 1) * T], p1[:, 2 * j + i, :], ident[0:T, 0:T])
                last.then_inc(done["p1T"], 1)

            def z1(j):
                eng.wait_ge(done["p1Tc"], j + 1)
                eng.wait_ge(done["vc"], j + 1)
                ps = take_bank(eng, "z1", j)
                for i in range(2):
                    last = mm(ps[0:T, i * D:(i + 1) * D], p1T[:, 2 * j + i, :], vbuf[:, 2 * j + i, :],
                              start=True, stop=True)
                last.then_inc(done["z1"], 1)

            def e2(b):
                eng.wait_ge(done["g2Tc"], b // 2 + 1)
                eng.wait_ge(d_ck[b // 2], 32)
                ps = take_bank(eng, "e2", b)
                for k in range(KD):
                    last = mm(ps[0:T, 0:S], featB[:, k, toks(b)], context(b // 2)[1][:, b % 2, k, :],
                              start=(k == 0), stop=(k == KD - 1))
                last.then_inc(done["e2"], 1)

            def len2(b):
                eng.wait_ge(done["cnt2"], b + 1)
                mm(bank("e2", b)[0:T, 400:401], cst[0:1, C_ONES:C_ONES + T], cnt[0:1, 1, b:b + 1],
                   start=True, stop=True).then_inc(done["len2"], 1)

            def p2T_(b):
                eng.wait_ge(done["exp2"], b + 1)
                ps = take_bank(eng, "p2T", b)
                for c in range(KS):
                    last = nc.tensor.transpose(ps[:, c * T:(c + 1) * T], p2[:, b % 4, c * P:(c + 1) * P],
                                               ident[0:T, 0:T])
                last.then_inc(done["p2T"], 1)

            def u_(j):
                eng.wait_ge(done["p2Tc"], 2 * j + 2)
                ps = take_bank(eng, "u", j)
                for i in range(2):
                    b = 2 * j + i
                    for c in range(KS):
                        last = mm(ps[0:T, i * D:(i + 1) * D], p2T[:, b % 4, c, :], context(j)[0][:, i, c, :],
                                  start=(c == 0), stop=(c == KS - 1))
                last.then_inc(done["u"], 1)

            def three(ps, a_hi, a_lo, b_hi, b_lo, first, last):
                mm(ps, a_hi, b_hi, start=first, stop=False)
                mm(ps, a_hi, b_lo, start=False, stop=False)
                return mm(ps, a_lo, b_hi, start=False, stop=last)

            def shared_up(name, which):
                def f(n):
                    g, f_ = n // KF, n % KF
                    eng.wait_ge(done["hlo"], 2 * g + 2)
                    eng.wait_ge(done["slo"], 2 * KD)
                    ps = take_bank(eng, name, n)
                    cols = slice(4 * T * g, 4 * T * (g + 1))
                    for k in range(KD):
                        w0 = which * KD * F + k * F + f_ * P
                        last = three(ps[:, 0:4 * T], ws_hi[:, w0:w0 + P], ws_lo[:, w0:w0 + P], hhi[:, k, cols],
                                     hlo[:, k, cols], k == 0, k == KD - 1)
                    last.then_inc(done[name], 1)
                return f

            def sd(j):
                eng.wait_ge(done["hsl"], KF * (j // 2 + 1))
                eng.wait_ge(done["slo"], 3 * KD)
                ps = take_bank(eng, "sd", j)
                for i in range(2):
                    for f in range(KF):
                        w = slice(2 * KD * F + f * D, 2 * KD * F + (f + 1) * D)
                        c = toks((2 * j + i) % 4)
                        last = three(ps[0:T, i * D:(i + 1) * D], hs_hi[j // 2][:, f, c], hs_lo[j // 2][:, f, c],
                                     ws_hi[:, w], ws_lo[:, w], f == 0, f == KF - 1)
                last.then_inc(done["sd"], 1)

            def lg(_):
                eng.wait_ge(done["hTc"], PAIRS)
                eng.wait_ge(d_gate, 16)
                ps = take_bank(eng, "lg", 0)
                for b in range(B):
                    for k in range(KD):
                        last = mm(ps[0:T, b * E:(b + 1) * E], featA[:, k, toks(b)], gate_sb[:, k, :],
                                  start=(k == 0), stop=(k == KD - 1))
                last.then_inc(done["lg"], 1)

            def scT(_):
                eng.wait_ge(done["score"], 1)
                ps = take_bank(eng, "scT", 0)
                nc.tensor.transpose(ps[:, 0:T], score.rearrange("t b e -> t (b e)"),
                                    ident[0:T, 0:T]).then_inc(done["scT"], 1)

            def bc(j):
                eng.wait_ge(done["dix"], 1)
                eng.wait_ge(done["const"], 1)
                ps = take_bank(eng, "bc", j)
                for i in range(2):
                    last = mm(ps[0:T, i * EC:(i + 1) * EC], bsel[:, 2 * j + i, :],
                              dix[:].rearrange("p e c -> p (e c)"), start=True, stop=True)
                last.then_inc(done["bc"], 1)

            def col(_):
                eng.wait_ge(done["dix"], 1)
                eng.wait_ge(done["const"], 1)
                ps = take_bank(eng, "col", 0)
                for hf in range(2):
                    c = slice(hf * HALF * CAP, (hf + 1) * HALF * CAP)
                    last = mm(ps[0:HALF * CAP, hf * B:(hf + 1) * B], dix[:].rearrange("p e c -> p (e c)")[:, c],
                              bcol[:], start=True, stop=True)
                last.then_inc(done["col"], 1)

            def slot(_):
                eng.wait_ge(done["top3"], 1)
                ps = take_bank(eng, "slot", 0)
                mm(ps[0:SLOTS, 0:E], top3[:].rearrange("p c b -> p (c b)"), cst[:, C_EMASK:C_EMASK + E],
                   start=True, stop=True).then_inc(done["slot"], 1)

            def gather(name, m):
                def f(j):
                    eng.wait_ge(done["sel"], j + 1)
                    eng.wait_ge(done["nm4"], j + 1)
                    ps = take_bank(eng, name, j)
                    for i in range(2):
                        b = 2 * j + i
                        last = mm(ps[:, i * EC:(i + 1) * EC], xn[:, b, m * P:(m + 1) * P], sel[:, b, :],
                                  start=True, stop=True)
                    last.then_inc(done[name], 1)
                return f

            def expert_up(name, which):
                def f(e):
                    if e == 0:
                        for m in range(KD):
                            eng.wait_ge(done[f"xgl{m}"], PAIRS)
                    eng.wait_ge(done["wl" + name], e + 1)
                    ps = take_bank(eng, name, e)
                    for k in range(KD):
                        w = slice(which * KD * F + k * F, which * KD * F + (k + 1) * F)
                        last = three(ps[0:SLOTS, 0:F], xgh[:, k, e, :], xgl[:, k, e, :], whi[e % 2][:, w],
                                     we_lo[:, e % RING, w], k == 0, k == KD - 1)
                    last.then_inc(done[name], 1)
                return f

            def hET(e):
                eng.wait_ge(done["hE"], e + 1)
                ps = take_bank(eng, "hET", e)
                for f in range(KF):
                    last = nc.tensor.transpose(ps[:, f * SLOTS:(f + 1) * SLOTS], hE[:, e % 2, f * P:(f + 1) * P],
                                               ident[0:SLOTS, 0:SLOTS])
                last.then_inc(done["hET"], 1)

            def down(e):
                eng.wait_ge(done["hEl"], e + 1)
                eng.wait_ge(done["wlD"], e + 1)
                ps = take_bank(eng, "D", e)
                for f in range(KF):
                    w = slice(2 * KD * F + f * D, 2 * KD * F + (f + 1) * D)
                    c = slice(f * SLOTS, (f + 1) * SLOTS)
                    last = three(ps[0:SLOTS, 0:D], hTh[:, e % 2, c], hTl[:, e % 2, c], whi[e % 2][:, w],
                                 we_lo[:, e % RING, w], f == 0, f == KF - 1)
                last.then_inc(done["D"], 1)

            def scat(n):
                hf, j = n // PAIRS, n % PAIRS
                for r in range(2):
                    eng.wait_ge(d_mv[r], 16 * (hf + 1) * (HALF // 2))
                eng.wait_ge(done["wsel"], 1)
                ps = take_bank(eng, "scat", n)
                for i in range(2):
                    b = 2 * j + i
                    last = mm(ps[0:T, i * D:(i + 1) * D], wsel[:, hf, b, :], eo_all[:, hf, b, :],
                              start=True, stop=True)
                last.then_inc(done["scat"], 1)

            def warm_up():
                eng.wait_ge(s_warm, 1)
                for _ in range(8):
                    mm(psum[:, BANKS - 1, :], warm[:, 0:P], warm[:], start=True, stop=True)

            warm_up()
            do = dict(m1=fused_weights("m1", W_Q1T, W_K1T, d_w1), m2=fused_weights("m2", W_Q2T, W_K2T, d_w2),
                      xT=turn("xT", xn, "nm0"), gT=by_feature("gT", m1, featA, "xTc", (done["m1c"], 1)),
                      v=by_token("v", featA, wsm[:, W_V1], "xTc"), e1=e1, len1=len1, p1T=p1T_, z1=z1,
                      x1T=turn("x1T", rn[:, 1], "nm1"),
                      g2T=by_feature("g2T", m2, featA, "x1Tc", (done["m2c"], 1)), e2=e2, len2=len2, p2T=p2T_,
                      u=u_, uT=turn("uT", u, "uc"), z2=by_token("z2", uT, wsm[:, W_V2], "uTc"),
                      x2T=turn("x2T", rn[:, 1], "nm2"), f1=by_feature("f1", wsm[:, W_FC1], featA, "x2Tc"),
                      f2=by_token("f2", featB, wsm[:, W_FC2], "f1c"), hT=turn("hT", xn, "nm4"),
                      shG=shared_up("shG", 0), shU=shared_up("shU", 1), sd=sd, lg=lg, scT=scT, bc=bc, col=col,
                      ga0=gather("ga0", 0), ga1=gather("ga1", 1), G=expert_up("G", 0), U=expert_up("U", 1), hET=hET, D=down, slot=slot, scat=scat)
            for name, unit in tensor_order:
                do[name](unit)

        @block.scalar
        def _(eng):
            act = nc.scalar.activation

            def fused_copy(name, dst):
                def f(_):
                    eng.wait_ge(done[name[:-1]], 1)
                    nc.scalar.copy(dst.rearrange("p k d -> p (k d)"), bank(name[:-1], 0)).then_inc(done[name], 1)
                return f

            def copy_pair(name, dst):
                def f(j):
                    eng.wait_ge(done[name], j + 1)
                    nc.scalar.copy(dst[:, :, pair_cols(j)],
                                   bank(name, j)[:, 0:4 * T].rearrange("p (k t) -> p k t", k=KD)
                                   ).then_inc(done[name + "c"], 1)
                return f

            def affine_pair(name, dst, func, bias, scale):
                def f(j):
                    eng.wait_ge(done[name], j + 1)
                    for k in range(KD):
                        last = act(dst[:, k, pair_cols(j)], bank(name, j)[:, 2 * k * T:2 * (k + 1) * T], func,
                                   bias=cst[:, bias + k:bias + k + 1],
                                   scale=cst[:, scale + k:scale + k + 1] if scale else 1.0)
                    last.then_inc(done[name + "c"], 1)
                return f

            def exp1(j):
                eng.wait_ge(done["mask1"], j + 1)
                for i in range(2):
                    b = 2 * j + i
                    last = act(p1[:, b, :], emk1[:, i, :], ACT.Exp, bias=nmax[:, 0, b:b + 1], scale=-1.0,
                               accum_out=rsum[:, 0, b:b + 1])
                last.then_inc(done["exp1"], 1)

            def p1Tc(j):
                eng.wait_ge(done["p1T"], j + 1)
                nc.scalar.copy(p1T[:, pair(j), :], bank("p1T", j)[0:T, 0:2 * T].rearrange("p (i t) -> p i t", i=2)
                               ).then_inc(done["p1Tc"], 1)

            def vc(j):
                eng.wait_ge(done["v"], j + 1)
                nc.scalar.copy(vbuf[:, pair(j), :], bank("v", j)[0:T, :].rearrange("p (i d) -> p i d", i=2)
                               ).then_inc(done["vc"], 1)

            def exp2(b):
                eng.wait_ge(done["mask2"], b + 1)
                if b == 0:
                    eng.wait_ge(done["const"], 1)
                if b >= 4:
                    eng.wait_ge(done["p2T"], b - 3)
                act(p2[:, b % 4, 0:S], emk[:, b % 2, :], ACT.Exp, bias=nmax[:, 1, b:b + 1], scale=-1.0,
                    accum_out=rsum[:, 1, b:b + 1]).then_inc(done["exp2"], 1)

            def p2Tc(b):
                eng.wait_ge(done["p2T"], b + 1)
                if b >= 4:
                    eng.wait_ge(done["u"], (b - 4) // 2 + 1)
                nc.scalar.copy(p2T[:, b % 4], bank("p2T", b)[:, 0:KS * T].rearrange("p (c t) -> p c t", c=KS)
                               ).then_inc(done["p2Tc"], 1)

            def uc(j):
                eng.wait_ge(done["u"], j + 1)
                eng.wait_ge(done["inv2"], j + 1)
                for i in range(2):
                    b = 2 * j + i
                    last = act(u[:, b, :], bank("u", j)[0:T, i * D:(i + 1) * D], ACT.Copy,
                               scale=rinv[:, 1, b:b + 1])
                last.then_inc(done["uc"], 1)

            def lex_(_):
                eng.wait_ge(done["lsh"], 1)
                act(lex, lsh, ACT.Exp).then_inc(done["lex"], 1)

            def gel_(n):
                eng.wait_ge(done["shG"], n + 1)
                if n == 0:
                    eng.wait_ge(done["z1"], PAIRS)
                if n >= 4:
                    eng.wait_ge(done["hsl"], n - 3)
                act(gel_s[:, n % 4, :], bank("shG", n)[:, 0:4 * T], ACT.Gelu).then_inc(done["gel"], 1)

            def hsh(n):
                g, f_ = n // KF, n % KF
                eng.wait_ge(done["hs"], n + 1)
                if n == 0:
                    eng.wait_ge(done["sum2"], PAIRS)
                if n == KF:
                    eng.wait_ge(done["x3"], PAIRS)
                nc.scalar.copy(hs_hi[g][:, f_, :], gel_s[:, n % 4, :]).then_inc(done["hsh"], 1)

            def hhi_(j):
                eng.wait_ge(done["hTc"], j + 1)
                if j == 0:
                    eng.wait_ge(done["z2"], PAIRS)
                nc.scalar.copy(hhi[:, :, pair_cols(j)], featA[:, :, pair_cols(j)]).then_inc(done["hhi"], 1)

            def shi(c):
                if c == 0:
                    eng.wait_ge(d_sh, 16)
                    eng.wait_ge(done["u"], PAIRS)
                    eng.wait_ge(done["e2"], B)
                nc.scalar.copy(ws_hi[:, c * F:(c + 1) * F], wshared[:, c * F:(c + 1) * F]).then_inc(done["shi"], 1)

            def xgh_(m):
                def f(j):
                    eng.wait_ge(done[f"ga{m}"], j + 1)
                    if j == 0:
                        eng.wait_ge(done["u"], 2)
                    nc.scalar.copy(xgh[:, m].rearrange("p e (c b) -> p e c b", b=B)[:, :, :, pair(j)],
                                   bank(f"ga{m}", j)[:, 0:2 * EC].rearrange("p (i e c) -> p e c i", i=2, e=E)
                                   ).then_inc(done[f"xgh{m}"], 1)
                return f

            def wh(part):
                cols = part_cols(part)

                def f(e):
                    eng.wait_ge((d_down if part == "D" else d_up)[e % RING], 16 * (e // RING + 1))
                    if e == 0:
                        eng.wait_ge(done["f2"], PAIRS)
                    elif e == 1:
                        eng.wait_ge(done["x3"], PAIRS)
                        eng.wait_ge(done["p2T"], B)
                    else:
                        eng.wait_ge(done[part], e - 1)
                    nc.scalar.copy(whi[e % 2][:, cols], we[:, e % RING, cols]).then_inc(done["wh" + part], 1)
                return f

            def gelE(e):
                eng.wait_ge(done["G"], e + 1)
                if e >= 2:
                    eng.wait_ge(done["hE"], e - 1)
                else:
                    eng.wait_ge(done["hsl"], 2 * KF)
                act(gel[0:SLOTS, e % 2, :], bank("G", e)[0:SLOTS, 0:F], ACT.Gelu).then_inc(done["gelE"], 1)

            def hEh(e):
                eng.wait_ge(done["hET"], e + 1)
                if e >= 2:
                    eng.wait_ge(done["D"], e - 1)
                else:
                    eng.wait_ge(done["shG"], 2 * KF)
                    eng.wait_ge(done["shU"], 2 * KF)
                nc.scalar.copy(hTh[:, e % 2, :], bank("hET", e)[:, 0:KF * SLOTS]).then_inc(done["hEh"], 1)

            def eo_(e):
                eng.wait_ge(done["D"], e + 1)
                if e >= 2:
                    eng.wait_ge(d_mv[e % 2], 16 * (e // 2))
                else:
                    eng.wait_ge(done["score3"], 1)
                act(eo[:, e % 2, :], bank("D", e)[0:SLOTS, 0:D], ACT.Copy,
                    scale=score3[:, e:e + 1]).then_inc(done["eo"], 1)

            do = dict(m1c=fused_copy("m1c", m1), m2c=fused_copy("m2c", m2), xTc=copy_pair("xT", featA),
                      gTc=copy_pair("gT", featB), vc=vc, exp1=exp1, p1Tc=p1Tc,
                      x1Tc=affine_pair("x1T", featA, ACT.Identity, V_B1, V_G1), g2Tc=copy_pair("g2T", featB),
                      exp2=exp2, p2Tc=p2Tc, uc=uc, uTc=copy_pair("uT", uT),
                      x2Tc=affine_pair("x2T", featA, ACT.Identity, V_B2, V_G2),
                      f1c=affine_pair("f1", featB, ACT.Relu, V_FC1, None), hTc=copy_pair("hT", featA),
                      lex=lex_, gel=gel_, hsh=hsh, hhi=hhi_, shi=shi, xgh0=xgh_(0), xgh1=xgh_(1),
                      whG=wh("G"), whU=wh("U"), whD=wh("D"), gelE=gelE,
                      hEh=hEh, eo=eo_)
            for name, unit in scalar_order:
                do[name](unit)

        @block.vector
        def _(eng):
            v_ = nc.vector
            chain = [0]

            def then(ins):
                chain[0] += 1
                ins.then_inc(k_dve, 1)
                eng.wait_ge(k_dve, chain[0])

            def stats(n, j, src, name):
                for i in range(2):
                    last = v_.bn_stats(st6[:, n, 2 * j + i, :], src[:, 2 * j + i, :])
                then(last)
                for i in range(2):
                    last = v_.bn_aggr(mv[:, n, 2 * j + i, :], st6[:, n, 2 * j + i, :])
                last.then_inc(done[name], 1)

            def nm(n, dst, src):
                def f(j):
                    eng.wait_ge(done[f"rs{n}"], j + 1)
                    for b in (2 * j, 2 * j + 1):
                        last = v_.tensor_scalar(dst[:, b, :], src[:, b, :], mv[:, n, b, 0:1], rstd[:, n, b, :],
                                                ALU.subtract, ALU.mult)
                    last.then_inc(done[f"nm{n}"], 1)
                return f

            def st0(j):
                eng.wait_ge(d_x[j], 16)
                stats(0, j, xres, "st0")

            counted = [None]

            def count(a, b, energies, name, value, signal):
                if counted[0]:
                    eng.wait_ge(*counted[0])
                n = energies.shape[-1]
                ins = v_.tensor_scalar(nz[0:1, 0:n], energies, 0.0, None, ALU.not_equal, ALU.add,
                                       accum_out=cnt[0:1, a, b:b + 1])
                if signal:
                    ins.then_inc(done[name], 1)
                    counted[0] = (done[name], value)
                else:
                    then(ins)
                    counted[0] = None

            def cnt1(j):
                eng.wait_ge(done["e1"], j + 1)
                for i in range(2):
                    count(0, 2 * j + i, bank("e1", j)[0:1, i * T:(i + 1) * T], "cnt1", j + 1, i == 1)

            def cnt2(b):
                eng.wait_ge(done["e2"], b + 1)
                count(1, b, bank("e2", b)[0:1, 0:S], "cnt2", b + 1, True)

            def mask(a, b, energies, length, key, pn, em):
                v_.reciprocal(linv[:, a, b:b + 1], length)
                then(v_.tensor_scalar(pn, key, length, FAR, ALU.is_ge, ALU.mult))
                return v_.tensor_tensor_reduce(em, energies, pn, -INV_SQRT_DK, 3.0e38, ALU.add, ALU.min,
                                               nmax[:, a, b:b + 1])

            def mask1(j):
                eng.wait_ge(done["len1"], j + 1)
                if j == 0:
                    eng.wait_ge(d_cst, 16)
                else:
                    eng.wait_ge(done["exp1"], j)
                ps = bank("e1", j)
                for i in range(2):
                    last = mask(0, 2 * j + i, ps[0:T, i * T:(i + 1) * T], ps[0:T, 400 + i:401 + i],
                                cst[0:T, C_CAUSAL:C_CAUSAL + T], pen1[:, i, :], emk1[:, i, :])
                last.then_inc(done["mask1"], 1)

            def mask2(b):
                eng.wait_ge(done["len2"], b + 1)
                if b >= 2:
                    eng.wait_ge(done["exp2"], b - 1)
                ps = bank("e2", b)
                mask(1, b, ps[0:T, 0:S], ps[0:T, 400:401], cst[0:T, C_KEY:C_KEY + S], pen[:, b % 2, :],
                     emk[:, b % 2, :]).then_inc(done["mask2"], 1)

            def const(_):
                v_.memset(p2[:, :, S:SP_], 0.0)
                eng.wait_ge(d_cst, 16)
                v_.tensor_copy(bcol[:], cst[:, C_BATCH:C_BATCH + B])
                v_.tensor_copy(bsel[:], cst[:, C_BATCH:C_BATCH + B].unsqueeze(2).to_broadcast([P, B, T])
                               ).then_inc(done["const"], 1)

            def inv(a, name, ready):
                def f(j):
                    eng.wait_ge(*ready(j))
                    c = pair(j)
                    then(v_.reciprocal(rinv[:, a, c], rsum[:, a, c]))
                    v_.scalar_tensor_tensor(rinv[:, a, c], linv[:, a, c], 0.0, rinv[:, a, c], ALU.mult,
                                            ALU.add).then_inc(done[name], 1)
                return f

            def sum1(j):
                eng.wait_ge(done["inv1"], j + 1)
                eng.wait_ge(done["z1"], j + 1)
                for i in range(2):
                    b = 2 * j + i
                    last = v_.scalar_tensor_tensor(rn[:, 0, b, :], bank("z1", j)[0:T, i * D:(i + 1) * D],
                                                   rinv[:, 0, b:b + 1], xn[:, b, :], ALU.mult, ALU.add)
                then(last)
                stats(1, j, rn[:, 0], "sum1")

            def plain_sum(name, n, product, res, ready):
                def f(j):
                    eng.wait_ge(done[product], j + 1)
                    eng.wait_ge(done[ready], j + 1)
                    then(v_.tensor_tensor(rn[:, 0, pair(j), :],
                                          bank(product, j)[0:T, :].rearrange("p (i d) -> p i d", i=2),
                                          res[:, pair(j), :], ALU.add))
                    stats(n, j, rn[:, 0], name)
                return f

            def x3(j):
                eng.wait_ge(done["x3m"], j + 1)
                eng.wait_ge(done["xb"], j + 1)
                v_.tensor_tensor(xres[:, pair(j), :], xres[:, pair(j), :], rn[:, 1, pair(j), :],
                                 ALU.add).then_inc(done["x3"], 1)

            def st4(j):
                eng.wait_ge(done["x3"], j + 1)
                stats(4, j, xres, "st4")

            def hlo_(j):
                eng.wait_ge(done["hhi"], j + 1)
                if j == 0:
                    eng.wait_ge(done["u"], PAIRS)
                    eng.wait_ge(done["exp2"], B)
                v_.tensor_tensor(hlo[:, :, pair_cols(j)], featA[:, :, pair_cols(j)],
                                 hhi[:, :, pair_cols(j)].bitcast(F32), ALU.subtract).then_inc(done["hlo"], 1)

            def slo(c):
                eng.wait_ge(done["shi"], c + 1)
                cols = slice(c * F, (c + 1) * F)
                v_.tensor_tensor(ws_lo[:, cols], wshared[:, cols], ws_hi[:, cols].bitcast(F32),
                                 ALU.subtract).then_inc(done["slo"], 1)

            def hs_(n):
                eng.wait_ge(done["gel"], n + 1)
                eng.wait_ge(done["shU"], n + 1)
                v_.tensor_tensor(gel_s[:, n % 4, :], gel_s[:, n % 4, :], bank("shU", n)[:, 0:4 * T],
                                 ALU.mult).then_inc(done["hs"], 1)

            def hsl(n):
                g, f_ = n // KF, n % KF
                eng.wait_ge(done["hsh"], n + 1)
                if n == 0:
                    eng.wait_ge(done["f2"], PAIRS)
                v_.tensor_tensor(hs_lo[g][:, f_, :], gel_s[:, n % 4, :], hs_hi[g][:, f_, :].bitcast(F32),
                                 ALU.subtract).then_inc(done["hsl"], 1)

            def add_to_result(ps, j, name):
                v_.tensor_tensor(xres[:, pair(j), :], ps[0:T, :].rearrange("p (i d) -> p i d", i=2),
                                 xres[:, pair(j), :], ALU.add).then_inc(done[name], 1)

            def y(j):
                eng.wait_ge(done["sd"], j + 1)
                add_to_result(bank("sd", j), j, "y")

            def fin(n):
                hf, j = n // PAIRS, n % PAIRS
                eng.wait_ge(done["scat"], n + 1)
                if hf == 0:
                    eng.wait_ge(done["y"], j + 1)
                else:
                    eng.wait_ge(done["fin"], j + 1)
                add_to_result(bank("scat", n), j, "fin")

            def lsh_(_):
                eng.wait_ge(done["lg"], 1)
                lg = bank("lg", 0)[0:T, 0:B * E].rearrange("p (b e) -> p b e", b=B)
                then(v_.tensor_reduce(lmx[:], lg, AX.X, ALU.max))
                v_.tensor_tensor(lsh, lg, lmx[:].unsqueeze(2).to_broadcast([T, B, E]),
                                 ALU.subtract).then_inc(done["lsh"], 1)

            def score_(_):
                eng.wait_ge(done["lex"], 1)
                then(v_.tensor_reduce(lsum[:], lex, AX.X, ALU.add))
                then(v_.reciprocal(lri[:], lsum[:]))
                v_.tensor_tensor(score, lex, lri[:].unsqueeze(2).to_broadcast([T, B, E]),
                                 ALU.mult).then_inc(done["score"], 1)

            def sc(_):
                eng.wait_ge(done["scT"], 1)
                v_.tensor_copy(sS[:], bank("scT", 0)[:, 0:T]).then_inc(done["sc"], 1)

            def dix_(_):
                eng.wait_ge(done["sc"], 1)
                then(v_.max(top[:, 0:8], sS[:]))
                v_.max_index(tix[:, 0:8], top[:, 0:8], sS[:])
                then(v_.match_replace(sS2[:], top[:, 0:8], sS[:], -1.0))
                then(v_.max(top[:, 8:16], sS2[:]))
                then(v_.max_index(tix[:, 8:16], top[:, 8:16], sS2[:]))
                then(v_.tensor_copy(tixf[:], tix[:]))
                em = cst[:, C_EMASK:C_EMASK + E].unsqueeze(2).to_broadcast([P, E, CAP])
                v_.tensor_tensor(dix[:], em, tixf[:, 0:CAP].unsqueeze(1).to_broadcast([P, E, CAP]),
                                 ALU.mult).then_inc(done["dix"], 1)

            def sel_(j):
                eng.wait_ge(done["bc"], j + 1)
                v_.tensor_scalar(sel[:, pair(j), :],
                                 bank("bc", j)[0:T, 0:2 * EC].rearrange("p (i c) -> p i c", i=2),
                                 cst[0:T, C_ROW:C_ROW + 1], None, ALU.is_equal).then_inc(done["sel"], 1)

            def top3_(_):
                v_.tensor_tensor(top3[:], top[:, 0:CAP].unsqueeze(2).to_broadcast([P, CAP, B]),
                                 cst[:, C_BATCH:C_BATCH + B].unsqueeze(1).to_broadcast([P, CAP, B]),
                                 ALU.mult).then_inc(done["top3"], 1)

            def score3_(_):
                eng.wait_ge(done["slot"], 1)
                v_.tensor_copy(score3[:], bank("slot", 0)[0:SLOTS, 0:E]).then_inc(done["score3"], 1)

            def wcol_(_):
                eng.wait_ge(done["col"], 1)
                v_.tensor_copy(wcol[:].rearrange("p h b -> p (h b)"),
                               bank("col", 0)[0:HALF * CAP, 0:2 * B]).then_inc(done["wcol"], 1)

            def wsel_(_):
                eng.wait_ge(done["wcol"], 1)
                eng.wait_ge(done["sd"], 2)
                for hf in range(2):
                    for b in range(B):
                        last = v_.tensor_scalar(wsel[:, hf, b, :], cst[0:HALF * CAP, C_KEY:C_KEY + T],
                                                wcol[:, hf, b:b + 1], None, ALU.is_equal)
                last.then_inc(done["wsel"], 1)

            def xgl_(m):
                def f(j):
                    eng.wait_ge(done[f"xgh{m}"], j + 1)

                    def cols(t):
                        return t[:, m].rearrange("p e (c b) -> p e c b", b=B)[:, :, :, pair(j)]

                    v_.tensor_tensor(cols(xgl), bank(f"ga{m}", j)[:, 0:2 * EC].rearrange(
                        "p (i e c) -> p e c i", i=2, e=E), cols(xgh).bitcast(F32),
                        ALU.subtract).then_inc(done[f"xgl{m}"], 1)
                return f

            def wl(part):
                cols = part_cols(part)

                def f(e):
                    eng.wait_ge(done["wh" + part], e + 1)
                    v_.tensor_tensor(we_lo[:, e % RING, cols], we[:, e % RING, cols],
                                     whi[e % 2][:, cols].bitcast(F32), ALU.subtract).then_inc(done["wl" + part], 1)
                return f

            def hE_(e):
                eng.wait_ge(done["gelE"], e + 1)
                eng.wait_ge(done["U"], e + 1)
                if e >= 2:
                    eng.wait_ge(done["hET"], e - 1)
                else:
                    eng.wait_ge(done["sd"], 2)
                v_.tensor_tensor(hE[:, e % 2, :], gel[0:SLOTS, e % 2, :], bank("U", e)[0:SLOTS, 0:F],
                                 ALU.mult).then_inc(done["hE"], 1)

            def hEl(e):
                eng.wait_ge(done["hEh"], e + 1)
                v_.tensor_tensor(hTl[:, e % 2, :], bank("hET", e)[:, 0:KF * SLOTS], hTh[:, e % 2, :].bitcast(F32),
                                 ALU.subtract).then_inc(done["hEl"], 1)

            do = dict(st0=st0, nm0=nm(0, xn, xres), cnt1=cnt1, mask1=mask1,
                      inv1=inv(0, "inv1", lambda j: (done["exp1"], j + 1)), sum1=sum1,
                      nm1=nm(1, rn[:, 1], rn[:, 0]), cnt2=cnt2, mask2=mask2,
                      inv2=inv(1, "inv2", lambda j: (done["exp2"], 2 * j + 2)),
                      sum2=plain_sum("sum2", 2, "z2", x1, "x1a"), nm2=nm(2, rn[:, 1], rn[:, 0]),
                      sum3=plain_sum("sum3", 3, "f2", vbuf, "x2a"), nm3=nm(3, rn[:, 1], rn[:, 0]), x3=x3, st4=st4,
                      nm4=nm(4, xn, xres), hs=hs_, y=y, fin=fin, lsh=lsh_, score=score_, sc=sc, dix=dix_,
                      const=const, sel=sel_, wcol=wcol_, wsel=wsel_, hsl=hsl, hlo=hlo_, slo=slo, top3=top3_, score3=score3_,
                      xgl0=xgl_(0), xgl1=xgl_(1), wlG=wl("G"), wlU=wl("U"), hE=hE_, hEl=hEl)
            v_.memset(warm[:], 0.0).then_inc(s_warm, 1)
            for name, unit in vector_order:
                do[name](unit)

        @block.gpsimd
        def _(eng):
            g_ = nc.gpsimd
            chain = [0]

            def then(ins):
                chain[0] += 1
                ins.then_inc(k_pool, 1)
                eng.wait_ge(k_pool, chain[0])

            def rs(n, ready):
                def f(j):
                    eng.wait_ge(done[ready], j + 1)
                    then(g_.tensor_scalar_add(ve[:, n, pair(j), :], mv[:, n, pair(j), 1:2], EPS))
                    g_.tensor_tensor(rstd[:, n, pair(j), :], ve[:, n, pair(j), :], nhalf[:],
                                     ALU.pow).then_inc(done[f"rs{n}"], 1)
                return f

            def affine(name, ready, dst, g, b):
                def f(j):
                    eng.wait_ge(done[ready], j + 1)
                    if name == "x1a" and j == 0:
                        eng.wait_ge(d_row, 16)
                    then(g_.tensor_tensor(dst[:, pair(j), :], rn[:, 1, pair(j), :], bcast_row(g), ALU.mult))
                    g_.tensor_tensor(dst[:, pair(j), :], dst[:, pair(j), :], bcast_row(b),
                                     ALU.add).then_inc(done[name], 1)
                return f

            fc2_bias = [False]

            def x2a(j):
                if not fc2_bias[0]:
                    fc2_bias[0] = True
                    then(g_.tensor_tensor(row[:, R_B2, :], row[:, R_B2, :], row[:, R_FC2, :], ALU.add))
                affine("x2a", "nm2", vbuf, R_G2, R_B2)(j)

            def xb(j):
                eng.wait_ge(done["nm0"], j + 1)
                if j == 0:
                    eng.wait_ge(d_row, 16)
                g_.tensor_tensor(xres[:, pair(j), :], xres[:, pair(j), :], bcast_row(R_B3),
                                 ALU.add).then_inc(done["xb"], 1)

            def x3m(j):
                eng.wait_ge(done["nm3"], j + 1)
                g_.tensor_tensor(rn[:, 1, pair(j), :], rn[:, 1, pair(j), :], bcast_row(R_G3),
                                 ALU.mult).then_inc(done["x3m"], 1)

            def wlD(e):
                eng.wait_ge(done["whD"], e + 1)
                cols = part_cols("D")
                g_.tensor_tensor(we_lo[:, e % RING, cols], we[:, e % RING, cols], whi[e % 2][:, cols].bitcast(F32),
                                 ALU.subtract).then_inc(done["wlD"], 1)

            then(g_.memset(nhalf[:], -0.5))
            do = dict(rs0=rs(0, "st0"), rs1=rs(1, "sum1"), x1a=affine("x1a", "nm1", x1, R_G1, R_B1),
                      rs2=rs(2, "sum2"), x2a=x2a, rs3=rs(3, "sum3"), xb=xb, x3m=x3m, rs4=rs(4, "st4"), wlD=wlD)
            for name, unit in pool_order:
                do[name](unit)


_NAMES = ("x", "ctx_tok", "ctx_feat", "w_small", "consts", "rows", "gate", "w_moe")


def kernel(**inputs):
    import numpy as _np
    import concourse.bacc as _bacc
    from concourse import mybir as _mybir
    from concourse.bass_utils import run_bass_kernel_spmd as _run

    a = {k: _np.asarray(v) for k, v in inputs.items()}
    f32 = _np.float32

    def chunked(w):
        return w.reshape(-1, P, w.shape[1]).transpose(1, 0, 2)

    def vec(v):
        return v.reshape(KD, P).T

    ctx = a["ctx_1024"]
    ctx_tok = _np.concatenate([ctx, _np.zeros((B, SP_ - S, D), f32)], axis=1)
    ctx_tok = ctx_tok.reshape(B, KS, P, D).transpose(2, 0, 1, 3)
    ctx_feat = ctx.reshape(B, S, KD, P).transpose(3, 0, 2, 1)
    w_small = _np.stack([chunked(w) for w in (
        a["L0_xattn_Wq1"].T, a["L0_xattn_Wk1"].T, a["L0_xattn_Wv1"], a["L0_xattn_Wq2"].T, a["L0_xattn_Wk2"].T,
        a["L0_xattn_Wv2"], a["L0_xattn_fc1_w"], a["L0_xattn_fc2_w"])], axis=1)
    part = _np.arange(P)
    key = _np.arange(S)
    causal = _np.where(key[None, :T] > part[:, None], 4 * S, key[None, :T])
    consts = _np.concatenate([
        _np.eye(P), causal, _np.broadcast_to(key, (P, S)), part[:, None],
        part[:, None] % E == _np.arange(E)[None], part[:, None] // E == _np.arange(B)[None],
        _np.ones((P, T))], axis=1).astype(f32)
    consts = _np.concatenate([consts] + [vec(a["L0_xattn_" + n]) for n in
                                         ("ln1_g", "ln1_b", "ln2_g", "ln2_b", "fc1_b")], axis=1)
    rows = _np.stack([a["L0_xattn_" + n] for n in ("ln1_g", "ln1_b", "ln2_g", "ln2_b", "ln3_g", "ln3_b", "fc2_b")])
    gate = chunked(a["L0_ffn_gate_w"].T)

    def moe(g, u, d):
        return _np.concatenate([chunked(w.T).reshape(P, -1) for w in (g, u, d)], axis=1)

    w_moe = _np.stack([moe(a["L0_ffn_Wg"][e], a["L0_ffn_Wu"][e], a["L0_ffn_Wd"][e]) for e in range(E)]
                      + [moe(a["L0_ffn_Ws_g"], a["L0_ffn_Ws_u"], a["L0_ffn_Ws_d"])])
    data = dict(x=a["x"], ctx_tok=ctx_tok, ctx_feat=ctx_feat, w_small=w_small, consts=consts, rows=rows,
                gate=gate, w_moe=w_moe)

    nc = _bacc.Bacc("TRN2", target_bir_lowering=False, num_devices=1)
    arrays, args = {}, []
    for name in _NAMES:
        arr = _np.ascontiguousarray(data[name])
        arrays[f"in_{name}"] = arr
        args.append(nc.dram_tensor(f"in_{name}", arr.shape, _mybir.dt.from_np(arr.dtype), kind="ExternalInput").ap())
    args.append(nc.dram_tensor("out_0", (B, T, D), F32, kind="ExternalOutput").ap())
    xattn_moe(nc, *args)
    r = _run(nc, [arrays], core_ids=[0])
    return r.results[0]["out_0"]
```
